# Optimizing a Trainium2 kernel written in Bass

```python
import numpy as np
import jax
import jax.numpy as jnp

def _softmax(x, axis=-1):
    return jax.nn.softmax(x, axis=axis)

def _gelu(x):
    return jax.nn.gelu(x, approximate=True)

def _silu(x):
    return jax.nn.silu(x)

def _sigmoid(x):
    return jax.nn.sigmoid(x)

def _layernorm(x, axis=-1, eps=1e-05):
    m = jnp.mean(x, axis=axis, keepdims=True)
    v = jnp.var(x, axis=axis, keepdims=True)
    return (x - m) / jnp.sqrt(v + eps)

def _scatter_add(tgt, idx, src, axis=0):
    return tgt.at[idx].add(src)

def _segment_sum(src, seg, n):
    return jax.ops.segment_sum(src, seg, n)
kernel_name = 'mk_gnn_ffn_d1_gnn_r8_005071'

def setup_inputs(seed: int=0):
    np.random.seed(seed)
    _w = jnp.asarray

    def _rec_inputs():
        import jax
        import jax.numpy as jnp
        _gk = jax.random.key(seed)
        x = -6.415e-05 + 1 * jax.random.normal(jax.random.fold_in(_gk, 1), (1250, 1024), jnp.float32)
        src = jax.random.randint(jax.random.fold_in(_gk, 2), (40000,), 0, 1250, jnp.int32)
        dst = jnp.minimum((1250 * jax.random.uniform(jax.random.fold_in(_gk, 3), (40000,)) ** 2.0).astype(jnp.int32), 9999)
        _o = jnp.argsort(dst, stable=True)
        src = src[_o]
        dst = dst[_o]
        edge_type_8 = jax.random.randint(jax.random.fold_in(_gk, 12), (40000,), 0, 8, jnp.int32)
        return (x, src, dst, edge_type_8)
    x, src, dst, edge_type_8 = _rec_inputs()

    def _L0_gnn_setup():
        import jax, jax.numpy as jnp
        import numpy as np
        N, D, R, E = (1250, 1024, 8, 10000)

        def _rgcn(x, edge_index, edge_type, weight, root, bias):
            src, dst = (edge_index[0], edge_index[1])
            msgs = x[src]
            out = x @ root + bias
            n = x.shape[0]
            for r in range(weight.shape[0]):
                mask = (edge_type == r).astype(x.dtype)
                sums = jax.ops.segment_sum(msgs * mask[:, None], dst, num_segments=n)
                cnt = jax.ops.segment_sum(mask, dst, num_segments=n)
                mean = sums / jnp.maximum(cnt, 1.0)[:, None]
                out = out + mean @ weight[r]
            return out
        key = jax.random.key(seed)
        ks = jax.random.split(key, 8)
        s = 1.0 / np.sqrt(D)
        x = jax.random.normal(ks[0], (N, D), dtype=jnp.float32)
        edge_index = jax.random.randint(ks[1], (2, E), 0, N, dtype=jnp.int64)
        edge_type = jax.random.randint(ks[2], (E,), 0, R, dtype=jnp.int64)
        weight = jax.random.normal(ks[3], (R, D, D), dtype=jnp.float32) * s
        root = jax.random.normal(ks[4], (D, D), dtype=jnp.float32) * s
        bias = jnp.zeros((D,), dtype=jnp.float32)
        w_gate = jax.random.normal(ks[5], (2 * D, D), dtype=jnp.float32) * (1.0 / np.sqrt(2 * D))
        b_gate = jnp.zeros((D,), dtype=jnp.float32)
        return {'x': x, 'edge_index': edge_index, 'edge_type': edge_type, 'weight': weight, 'root': root, 'bias': bias, 'w_gate': w_gate, 'b_gate': b_gate}
    _L0_gnn_all = _L0_gnn_setup()
    _L0_gnn_in = {k: v for k, v in _L0_gnn_all.items() if k in ('weight', 'root', 'bias', 'w_gate', 'b_gate')}
    del _L0_gnn_all

    def _L0_ffn_setup():
        import jax, jax.numpy as jnp
        import numpy as np
        B, S, D, F, E = (2, 256, 1024, 512, 8)
        LN_EPS = 1e-05

        def _layer_norm(x, gamma, beta):
            mu = jnp.mean(x, axis=-1, keepdims=True)
            var = jnp.mean(jnp.square(x - mu), axis=-1, keepdims=True)
            return (x - mu) * jax.lax.rsqrt(var + LN_EPS) * gamma + beta
        key = jax.random.key(seed)
        ks = jax.random.split(key, 8)

        def xavier(k, shape):
            fan_in, fan_out = (shape[-1], shape[-2])
            a = jnp.sqrt(6.0 / (fan_in + fan_out))
            return jax.random.uniform(k, shape, jnp.float32, -a, a)
        return {'tgt': jax.random.normal(ks[0], (B, S, D), jnp.float32), 'Wr': xavier(ks[1], (E, D)), 'br': jnp.zeros((E,), jnp.float32), 'W1': xavier(ks[2], (E, F, D)), 'b1': jnp.zeros((E, F), jnp.float32), 'W2': xavier(ks[3], (E, D, F)), 'b2': jnp.zeros((E, D), jnp.float32), 'gamma': jnp.ones((D,), jnp.float32), 'beta': jnp.zeros((D,), jnp.float32)}
    _L0_ffn_all = _L0_ffn_setup()
    _L0_ffn_in = {k: v for k, v in _L0_ffn_all.items() if k in ('Wr', 'br', 'W1', 'b1', 'W2', 'b2', 'gamma', 'beta')}
    del _L0_ffn_all
    return {'x': x, 'src': src, 'dst': dst, 'edge_type_8': edge_type_8, 'L0_gnn_weight': _L0_gnn_in['weight'], 'L0_gnn_root': _L0_gnn_in['root'], 'L0_gnn_bias': _L0_gnn_in['bias'], 'L0_gnn_w_gate': _L0_gnn_in['w_gate'], 'L0_gnn_b_gate': _L0_gnn_in['b_gate'], 'L0_ffn_Wr': _L0_ffn_in['Wr'], 'L0_ffn_br': _L0_ffn_in['br'], 'L0_ffn_W1': _L0_ffn_in['W1'], 'L0_ffn_b1': _L0_ffn_in['b1'], 'L0_ffn_W2': _L0_ffn_in['W2'], 'L0_ffn_b2': _L0_ffn_in['b2'], 'L0_ffn_gamma': _L0_ffn_in['gamma'], 'L0_ffn_beta': _L0_ffn_in['beta']}

def reference(x, src, dst, edge_type_8, L0_gnn_weight, L0_gnn_root, L0_gnn_bias, L0_gnn_w_gate, L0_gnn_b_gate, L0_ffn_Wr, L0_ffn_br, L0_ffn_W1, L0_ffn_b1, L0_ffn_W2, L0_ffn_b2, L0_ffn_gamma, L0_ffn_beta):
    import jax
    import jax.numpy as jnp

    def _L0_gnn_ref(x, edge_index, edge_type, weight, root, bias, w_gate, b_gate):
        import jax, jax.numpy as jnp
        import numpy as np
        N, D, R, E = (1250, 1024, 8, 10000)

        def _rgcn(x, edge_index, edge_type, weight, root, bias):
            src, dst = (edge_index[0], edge_index[1])
            msgs = x[src]
            out = x @ root + bias
            n = x.shape[0]
            for r in range(weight.shape[0]):
                mask = (edge_type == r).astype(x.dtype)
                sums = jax.ops.segment_sum(msgs * mask[:, None], dst, num_segments=n)
                cnt = jax.ops.segment_sum(mask, dst, num_segments=n)
                mean = sums / jnp.maximum(cnt, 1.0)[:, None]
                out = out + mean @ weight[r]
            return out
        u = _rgcn(x, edge_index, edge_type, weight, root, bias)
        z = jnp.concatenate([u, x], axis=1) @ w_gate + b_gate
        h = jnp.tanh(u) * z + x * (1.0 - z)
        return h

    def _L0_ffn_ref(tgt, Wr, br, W1, b1, W2, b2, gamma, beta):
        import jax, jax.numpy as jnp
        import numpy as np
        B, S, D, F, E = (2, 256, 1024, 512, 8)
        LN_EPS = 1e-05

        def _layer_norm(x, gamma, beta):
            mu = jnp.mean(x, axis=-1, keepdims=True)
            var = jnp.mean(jnp.square(x - mu), axis=-1, keepdims=True)
            return (x - mu) * jax.lax.rsqrt(var + LN_EPS) * gamma + beta
        logits = jnp.einsum('bsd,ed->bse', tgt, Wr) + br
        top_v, top_i = jax.lax.top_k(logits, 2)
        top_w = jax.nn.softmax(top_v, axis=-1)
        n_exp = logits.shape[-1]
        router_w = jnp.sum(jax.nn.one_hot(top_i, n_exp, dtype=top_w.dtype) * top_w[..., None], axis=-2)
        h = jnp.einsum('bsd,efd->bsef', tgt, W1) + b1
        h = jax.nn.relu(h)
        o = jnp.einsum('bsef,edf->bsed', h, W2) + b2
        tgt2 = jnp.einsum('bsed,bse->bsd', o, router_w)
        return _layer_norm(tgt + tgt2, gamma, beta)
    edge_index = jnp.stack([src, dst])
    x = x + _L0_gnn_ref(_layernorm(x, axis=-1), edge_index, edge_type_8, L0_gnn_weight, L0_gnn_root, L0_gnn_bias, L0_gnn_w_gate, L0_gnn_b_gate)
    x = x + _L0_ffn_ref(_layernorm(x, axis=-1)[None], L0_ffn_Wr, L0_ffn_br, L0_ffn_W1, L0_ffn_b1, L0_ffn_W2, L0_ffn_b2, L0_ffn_gamma, L0_ffn_beta)[0]
    return x

_drawn_inputs = setup_inputs


def setup_inputs(seed=0):
    import zlib

    import numpy as np

    out = dict(_drawn_inputs(seed))
    spreads = {'L0_gnn_bias': (0.0, 0.1),
     'L0_gnn_b_gate': (0.0, 0.1),
     'L0_ffn_br': (0.0, 0.1),
     'L0_ffn_b1': (0.0, 0.754),
     'L0_ffn_b2': (0.0, 0.426),
     'L0_ffn_gamma': (1.0, 0.2),
     'L0_ffn_beta': (0.0, 0.307)}
    factors = {}
    for name, (base, spread) in spreads.items():
        noise = np.random.default_rng([zlib.crc32(name.encode()), seed]).standard_normal(out[name].shape)
        drawn = base * np.exp(spread * noise) if base else spread * noise
        out[name] = jnp.asarray(drawn.astype(out[name].dtype))
    for name, factor in factors.items():
        out[name] = (out[name] * factor).astype(out[name].dtype)
    return out
```

```python
from contextlib import ExitStack

import concourse.bass as bass
import concourse.mybir as mybir
from concourse.bass import IndirectOffsetOnAxis

F32 = mybir.dt.float32
F32R = mybir.dt.float32r
F16 = mybir.dt.float16
I32 = mybir.dt.int32
ALU = mybir.AluOpType
ACT = mybir.ActivationFunctionType
AX = mybir.AxisListType

P = 128
N, D, R, E, F = 1250, 1024, 8, 8, 512
HALF = 512
TILES = -(-N // P)
KD = D // P
KF = F // P
EDGES, EP = 40000, 125
EC = EDGES // EP
GROUP = 4
GROUPS = (EDGES + TILES * (GROUP * P - 1)) // (GROUP * P)
BLOCKS = GROUPS * GROUP
BUCKETS = TILES * R
CHUNKS_R, CH_ROOT, CH_GATEX, CH_GATEU, CH_EXP = 2 * R, 2 * R, 2 * R + 2, 2 * R + 4, 2 * R + 6
CW = KD * HALF
PIECE = 1024
PIECES = CW // PIECE
EPS = 1e-5
Y_PAD = 1 << 20
COLS_PER_TILE = 4
INDEX_CHUNKS = EC // (TILES * COLS_PER_TILE)
TOKEN_CHUNKS = [(0, 4), (4, 8), (8, 10)]


def rows(m):
    return min(P, N - m * P)


def program(nc, x, src, dst, etype, wchunks, bias, b_gate, wr, br, b1, b2, gamma, beta, out):
    ctx = ExitStack()
    with ctx:
        def sb(name, shape, dt=F32):
            return ctx.enter_context(nc.sbuf_tensor(name, shape, dt))

        def sem(name):
            return ctx.enter_context(nc.semaphore(name))

        y_dram = nc.dram_tensor("y_rows", (R * N, D), F32, kind="Internal").ap()
        zx_dram = nc.dram_tensor("zx_rows", (N, D), F32, kind="Internal").ap()
        x1_dram = nc.dram_tensor("x1_rows", (N, D), F32, kind="Internal").ap()
        recip_dram = nc.dram_tensor("recip_table", (BUCKETS * P + P, 1), F32, kind="Internal").ap()

        w_hi = sb("w_hi", [P, 2, CW], F32R)
        w_lo = sb("w_lo", [P, 2, CW], F32R)
        w_raw = sb("w_raw", [P, 2, PIECE])
        acc = sb("acc", [P, TILES, D])
        ident = sb("ident", [P, P])
        mean_all = sb("mean_all", [P, TILES])
        rstd_all = sb("rstd_all", [P, TILES])
        router = sb("router", [P, TILES, E])
        b1_sb = sb("b1_sb", [P, E, KF])
        wr_raw = sb("wr_raw", [P, KD, E])
        wr_hi = sb("wr_hi", [P, KD, E], F32R)
        wr_lo = sb("wr_lo", [P, KD, E], F32R)
        br_bc = sb("br_bc", [P, E])
        stats = sb("stats", [P, 2, 2, 6])
        aggr = sb("aggr", [P, 2, 2])
        rs = sb("rs", [P, 2, 4])
        b1_here, w_here = sb("b1_here", [P, KF]), sb("w_here", [P, TILES])
        sorting = ctx.enter_context(ExitStack())

        def sort_sb(name, shape, dt=F32):
            return sorting.enter_context(nc.sbuf_tensor(name, shape, dt))

        sort_row = sort_sb("sort_row", [P, BLOCKS], I32)
        sort_local = sort_sb("sort_local", [P, BLOCKS])
        sort_recip = sort_sb("sort_recip", [P, BLOCKS])
        group_tile = sort_sb("group_tile", [P, GROUPS], I32)
        recip_at = sort_sb("recip_at", [P, BLOCKS], I32)
        gate_word = sort_sb("gate_word", [1, 2])
        l_slot_i, l_slot_r = sort_sb("l_slot_i", [P, 8], I32), sort_sb("l_slot_r", [P, 8])
        operands = ctx.enter_context(ExitStack())
        xnT_hi = operands.enter_context(nc.sbuf_tensor("xnT_hi", [P, KD, N], F32R))
        xnT_lo = operands.enter_context(nc.sbuf_tensor("xnT_lo", [P, KD, N], F32R))
        work = operands.enter_context(nc.sbuf_tensor("work", [P, 4096], F32))
        bank = [ctx.enter_context(nc.psum_tensor(f"bank{i}", [P, HALF], F32)) for i in range(8)]

        w_ready_hi, w_ready_lo = sem("w_ready_hi"), sem("w_ready_lo")
        w_loaded = [sem("w_loaded0"), sem("w_loaded1")]
        b1_copied, w_copied = sem("b1_copied"), sem("w_copied")

        def wait_after_first(eng, semaphore, count):
            if not isinstance(count, int) or count > 0:
                eng.wait_ge(semaphore, count)

        def norm_stats(v, link, of, a, rm, var_ready):
            for q in range(2):
                i = v.bn_stats(stats[:rm, a, q, :], of[:, q * HALF:(q + 1) * HALF])
            link(i)
            link(v.bn_aggr(aggr[:rm, a, :], stats[:rm, a, :, :]))
            v.tensor_scalar(rs[:rm, a, 0:1], aggr[:rm, a, 1:2], EPS, None, ALU.add).then_inc(var_ready, 1)

        def rstd(v, link, a, rm, to):
            s, root, r, w = (rs[:rm, a, k:k + 1] for k in range(4))
            link(v.reciprocal(r, root))
            link(v.tensor_tensor(w, r, r, ALU.mult))
            link(v.tensor_tensor(w, w, s, ALU.mult))
            link(v.tensor_scalar(w, w, -0.5, 1.5, ALU.mult, ALU.add))
            link(v.tensor_tensor(to, w, r, ALU.mult))

        xa = acc[:, 0:4, :]
        xn = acc[:, 4:8, :]
        with ExitStack() as stage:
            x_loaded = [stage.enter_context(nc.semaphore(f"x_loaded{i}")) for i in range(4)]
            def ssem(name):
                return stage.enter_context(nc.semaphore(name))
            std_ready, var_ready, xn_ready, t_done, hi_done, lo_done = (
                ssem("n_std"), ssem("n_var"), ssem("n_xn"), ssem("n_t"), ssem("n_hi"), ssem("n_lo"))
            id0, id1, vch = ssem("n_id0"), ssem("n_id1"), ssem("n_vch")
            block = stage.enter_context(nc.Block())

            @block.sync
            def _(sp):
                for m in range(TILES):
                    if m >= 4:
                        sp.wait_ge(xn_ready, m - 3)
                    sp.dma_start(xa[:rows(m), m % 4, :], x[m * P:m * P + rows(m), :])\
                        .then_inc(x_loaded[m % 4], 16)

            @block.gpsimd
            def _(pool):
                pool.memset(ident[:, :], 0.0).then_inc(id0, 1)
                pool.wait_ge(id0, 1)
                pool.affine_select(out=ident[:, :], in_=ident[:, :], compare_op=ALU.not_equal, fill=1.0,
                                   base=0, pattern=[[-1, P]], channel_multiplier=1).then_inc(id1, 1)

            @block.vector
            def _(v):
                n = [0]

                def link(ins):
                    n[0] += 1
                    ins.then_inc(vch, 1)
                    v.wait_ge(vch, n[0])

                def lo_parts(m):
                    for q in range(2):
                        v.wait_ge(hi_done, 2 * m + q + 1)
                        src_t = bank[2 * (m % 4) + q][:, :].rearrange("p (k n) -> p k n", k=4)[:, :, :rows(m)]
                        cols = slice(m * P, m * P + rows(m))
                        v.tensor_tensor(xnT_lo[:, 4 * q:4 * q + 4, cols], src_t,
                                        xnT_hi[:, 4 * q:4 * q + 4, cols].bitcast(F32), ALU.subtract)\
                            .then_inc(lo_done, 1)

                for m in range(TILES):
                    a, rm = m % 2, rows(m)
                    v.wait_ge(x_loaded[m % 4], 16 * (m // 4 + 1))
                    norm_stats(v, link, xa[:rm, m % 4, :], a, rm, var_ready)
                    link(v.tensor_copy(mean_all[:rm, m:m + 1], aggr[:rm, a, 0:1]))
                    v.wait_ge(std_ready, m + 1)
                    rstd(v, link, a, rm, rstd_all[:rm, m:m + 1])
                    if m >= 4:
                        v.wait_ge(t_done, m - 3)
                    v.tensor_scalar(xn[:rm, m % 4, :], xa[:rm, m % 4, :], mean_all[:rm, m:m + 1],
                                    rstd_all[:rm, m:m + 1], ALU.subtract, ALU.mult).then_inc(xn_ready, 1)
                    if m >= 1:
                        lo_parts(m - 1)
                lo_parts(TILES - 1)

            @block.scalar
            def _(act):
                def hi_parts(m):
                    act.wait_ge(t_done, m + 1)
                    for q in range(2):
                        src_t = bank[2 * (m % 4) + q][:, :].rearrange("p (k n) -> p k n", k=4)[:, :, :rows(m)]
                        act.activation(xnT_hi[:, 4 * q:4 * q + 4, m * P:m * P + rows(m)], src_t, ACT.Copy)\
                            .then_inc(hi_done, 1)
                for m in range(TILES):
                    a, rm = m % 2, rows(m)
                    act.wait_ge(var_ready, m + 1)
                    act.activation(rs[:rm, a, 1:2], rs[:rm, a, 0:1], ACT.Sqrt).then_inc(std_ready, 1)
                    if m >= 1:
                        hi_parts(m - 1)
                hi_parts(TILES - 1)

            @block.tensor
            def _(pe):
                pe.wait_ge(id1, 1)
                for m in range(TILES):
                    pe.wait_ge(xn_ready, m + 1)
                    if m >= 4:
                        pe.wait_ge(lo_done, 2 * (m - 3))
                    rm = rows(m)
                    for k in range(KD):
                        t = pe.transpose(bank[2 * (m % 4) + k // 4][:, (k % 4) * P:(k % 4) * P + rm],
                                         xn[:rm, m % 4, k * P:(k + 1) * P], ident[:rm, :rm])
                    t.then_inc(t_done, 1)
        index = acc[:, :, :].rearrange("p t d -> p (t d)")
        used = [0]

        def carve(words, dt=F32, parts=P):
            at = used[0]
            used[0] += words
            assert used[0] <= TILES * D
            ap = index[:parts, at:at + words]
            return ap if dt == F32 else ap.bitcast(dt)

        e_src, e_dst, e_type = (carve(EC, I32, EP) for _ in range(3))
        e_loc_i, e_tile_i = carve(EC, I32, EP), carve(EC, I32, EP)
        e_srcf, e_typef, e_loc, e_tile, e_key, e_bucket = (carve(EC, F32, EP) for _ in range(6))
        e_mask, e_scan, e_pos, e_p, e_j, e_ones = (carve(EC, F32, EP) for _ in range(6))
        e_totals = carve(TILES, F32, EP)
        t_count, t_groups, t_start, t_off = (carve(TILES) for _ in range(4))
        t_int = carve(TILES, I32)
        iota_i, iota_f = carve(BLOCKS, I32), carve(BLOCKS)
        iota_h = carve(BLOCKS // 2, F16)
        tri, ones = carve(P, F32, EP), carve(P, F32, EP)
        hot_p = carve(4 * P // 2, F16, EP).rearrange("p (s n) -> p s n", s=4)
        hot_src = carve(4 * BLOCKS // 2, F16, EP).rearrange("p (s n) -> p s n", s=4)
        hot_key = carve(4 * BLOCKS // 2, F16, EP).rearrange("p (s n) -> p s n", s=4)
        hot_bucket = carve(4 * BUCKETS // 2, F16, EP).rearrange("p (s n) -> p s n", s=4)
        hot_local = carve(4 * P // 2, F16, EP).rearrange("p (s n) -> p s n", s=4)
        free_at = [0]

        def again(words, dt=F32):
            at = free_at[0]
            free_at[0] += words
            assert free_at[0] <= 17 * EC
            ap = index[:, at:at + words]
            return ap if dt == F32 else ap.bitcast(dt)

        l_key, l_keyi, l_reli = again(BLOCKS), again(BLOCKS, I32), again(BLOCKS, I32)
        l_relf, l_row, l_pad, l_tile = (again(BLOCKS) for _ in range(4))
        l_at, l_loci = again(BLOCKS), again(BLOCKS, I32)
        l_recip = again(P)

        stage_y = work[:, 0:4 * HALF].rearrange("p (s n) -> p s n", s=4)
        bias_bc, gate_bc = work[:, 2048:3072], work[:, 3072:4096]
        first_ix = 2
        SRC_BANK, KEY_BANK, CNT_BANK = bank[5], bank[6], bank[7]

        with ExitStack() as stage:
            def ssem(name):
                return stage.enter_context(nc.semaphore(name))

            mm_done, evac_done, evac_v = ssem("p_mm"), ssem("p_evac"), ssem("p_evac_v")
            y_stored = [ssem(f"p_ystored{i}") for i in range(4)]
            edges_in, bias_in, index_ready, iota_done = ssem("p_edges"), ssem("p_bias"), ssem("p_ix"), ssem("p_iota")
            tri_done, totals_done, prefix_done = ssem("p_tri"), ssem("p_totals"), ssem("p_prefix")
            hot_ready, hot_used, vch = ssem("p_hot"), ssem("p_hotused"), ssem("p_vch")
            recip_made, recip_stored = ssem("p_recip"), ssem("p_recip_st")
            pool_ch, rg = ssem("p_poolch"), [ssem(f"p_rg{i}") for i in range(8)]
            block = stage.enter_context(nc.Block())

            def load_piece(sp, c, q, piece):
                sp.dma_start(w_raw[:, q % 2, :], wchunks[bass.ds(c * P, P), q * PIECE:(q + 1) * PIECE])\
                    .then_inc(w_loaded[q % 2], 16)

            def raw_free(sp, piece):
                sp.wait_ge(w_ready_hi, piece - 1)
                sp.wait_ge(w_ready_lo, piece - 1)

            @block.sync
            def _(sp):
                for q in range(2):
                    load_piece(sp, 0, q, q)
                for ap, of in ((e_src, src), (e_dst, dst), (e_type, etype)):
                    sp.dma_start(ap, of).then_inc(edges_in, 16)
                sp.dma_start(bias_bc, bias[0:1, :].to_broadcast([P, D])).then_inc(bias_in, 16)
                sp.dma_start(gate_bc, b_gate[0:1, :].to_broadcast([P, D])).then_inc(bias_in, 16)
                for q in range(2):
                    raw_free(sp, q + 2)
                    load_piece(sp, 0, q + 2, q + 2)
                for q in range(2):
                    raw_free(sp, 4 + q)
                    load_piece(sp, 1, q, 4 + q)

                def chunk(c, s, dest=None, prefetch=True):
                    for m in range(TILES):
                        t = TILES * s + m
                        if dest is not None:
                            sp.wait_ge(*dest[1](m))
                            sp.dma_start(dest[0](m), stage_y[:rows(m), t % 4, :]).then_inc(y_stored[t % 4], 16)
                        if m in (1, 3, 5, 7) and prefetch:
                            q = (m - 1) // 2 + 2
                            raw_free(sp, 4 * (c + 1) + q)
                            load_piece(sp, c + 1 + q // 4, q % 4, None)

                def y_dest(r, c, s):
                    return (lambda m: y_dram[bass.ds(r * N + m * P, rows(m)), s * HALF:(s + 1) * HALF],
                            lambda m: (evac_done, c * TILES + m + 1))

                for s in range(2):
                    chunk(s, s, y_dest(0, s, s))
                with sp.Fori(1, R) as r:
                    for s in range(2):
                        chunk(2 * r + s, s, y_dest(r, 2 * r + s, s))
                for s in range(2):
                    chunk(CH_ROOT + s, s)
                for s in range(2):
                    chunk(CH_GATEX + s, s,
                          (lambda m, s=s: zx_dram[m * P:m * P + rows(m), s * HALF:(s + 1) * HALF],
                           lambda m, s=s: (evac_v, (2 + s) * TILES + m + 1)), prefetch=(s == 0))
                for i in range(4):
                    sp.wait_ge(y_stored[i], 16 * 5 * (R + 1))

            def hi_piece(act, c, s, q):
                act.wait_ge(w_loaded[q % 2], 32 * c + 16 * (q // 2 + 1))
                act.activation(w_hi[:, s, q * PIECE:(q + 1) * PIECE], w_raw[:, q % 2, :], ACT.Copy)\
                    .then_inc(w_ready_hi, 1)

            def lo_piece(v, c, s, q):
                v.wait_ge(w_ready_hi, 4 * c + q + 1)
                v.tensor_tensor(w_lo[:, s, q * PIECE:(q + 1) * PIECE], w_raw[:, q % 2, :],
                                w_hi[:, s, q * PIECE:(q + 1) * PIECE].bitcast(F32), ALU.subtract)\
                    .then_inc(w_ready_lo, 1)

            @block.scalar
            def _(act):
                for q in range(4):
                    hi_piece(act, 0, 0, q)

                def chunk(c, s, evac=True, first=False, split=True):
                    for m in range(TILES):
                        t = TILES * s + m
                        act.wait_ge(mm_done, c * TILES + m + 1)
                        if evac:
                            if not (first and t < 4):
                                act.wait_ge(y_stored[t % 4], 16 * 5 * (c // 2 if isinstance(c, int) else r_of[0])
                                            + 16 * (t // 4))
                            act.activation(stage_y[:rows(m), t % 4, :], bank[t % 4][:rows(m), :], ACT.Copy)\
                                .then_inc(evac_done, 1)
                        if m in (1, 3, 5, 7) and split:
                            hi_piece(act, c + 1, 1 - s, (m - 1) // 2)

                r_of = [0]
                for s in range(2):
                    chunk(s, s, first=True)
                with act.Fori(1, R) as r:
                    r_of[0] = r
                    for s in range(2):
                        chunk(2 * r + s, s)
                for s in range(4):
                    chunk(CH_ROOT + s, s % 2, evac=False, split=s < 3)

            @block.tensor
            def _(pe):
                def prefix():
                    pe.wait_ge(totals_done, 1)
                    pe.matmul(CNT_BANK[:, 0:TILES], tri, e_totals, start=True, stop=True)
                    pe.matmul(CNT_BANK[:, TILES:2 * TILES], ones, e_totals, start=True, stop=True)\
                        .then_inc(prefix_done, 1)

                def column(col, slot, first, last):
                    pe.wait_ge(hot_ready, col + 1)
                    pe.matmul(SRC_BANK[:, 0:BLOCKS], hot_p[:, slot, :], hot_src[:, slot, :], start=first, stop=last)
                    pe.matmul(KEY_BANK[:, 0:BLOCKS], hot_p[:, slot, :], hot_key[:, slot, :], start=first, stop=last)
                    pe.matmul(CNT_BANK[:BUCKETS, 0:P], hot_bucket[:, slot, :], hot_local[:, slot, :],
                              start=first, stop=last).then_inc(hot_used, 1)

                def chunk(c, s, first=False, cols=None, from_v=False, ends=(False, False)):
                    pe.wait_ge(w_ready_hi, 4 * c + 4)
                    pe.wait_ge(w_ready_lo, 4 * c + 4)
                    for m in range(TILES):
                        t = TILES * s + m
                        rm = rows(m)
                        if from_v and (c > CH_ROOT or m >= 4):
                            pe.wait_ge(evac_v, (c - CH_ROOT) * TILES + m - 3)
                        elif not (first and t < 4):
                            pe.wait_ge(evac_done, c * TILES + m - 3)
                        n = 0
                        for a_, b_ in ((xnT_hi, w_hi), (xnT_hi, w_lo), (xnT_lo, w_hi)):
                            for k in range(KD):
                                i = pe.matmul(bank[t % 4][:rm, :], a_[:, k, m * P:m * P + rm],
                                              b_[:, s, k * HALF:(k + 1) * HALF], start=(n == 0), stop=(n == 3 * KD - 1))
                                n += 1
                        i.then_inc(mm_done, 1)
                        if cols is not None:
                            for q in range(COLS_PER_TILE):
                                column(cols + m * COLS_PER_TILE + q, q, ends[0] and m == 0 and q == 0,
                                       ends[1] and m == TILES - 1 and q == COLS_PER_TILE - 1)

                chunk(0, 0, first=True)
                prefix()
                chunk(1, 1, first=True)
                step = TILES * COLS_PER_TILE
                for s in range(2):
                    chunk(2 + s, s, cols=s * step, ends=(s == 0, False))
                with pe.Fori(1, INDEX_CHUNKS // 2 - 1) as i:
                    for s in range(2):
                        chunk(2 * i + 2 + s, s, cols=i * (2 * step) + s * step)
                for s in range(2):
                    c = INDEX_CHUNKS + s
                    chunk(c, s, cols=(c - 2) * step, ends=(False, s == 1))
                with pe.Fori(INDEX_CHUNKS // 2 + 1, R) as i:
                    for s in range(2):
                        chunk(2 * i + s, s)
                for s in range(4):
                    chunk(CH_ROOT + s, s % 2, from_v=True)

            @block.vector
            def _(v):
                n = [0]

                def link(ins):
                    n[0] += 1
                    ins.then_inc(vch, 1)
                    v.wait_ge(vch, n[0])

                for q in range(4):
                    lo_piece(v, 0, 0, q)
                v.wait_ge(edges_in, 48)
                v.tensor_copy(e_srcf, e_src)
                v.tensor_copy(e_typef, e_type)
                v.memset(e_ones, 1.0)
                v.tensor_scalar(e_loc_i, e_dst, P - 1, None, ALU.bitwise_and)
                link(v.tensor_scalar(e_tile_i, e_dst, P.bit_length() - 1, None, ALU.logical_shift_right))
                v.tensor_copy(e_loc, e_loc_i)
                v.tensor_copy(e_tile, e_tile_i)
                link(v.tensor_scalar(e_srcf, e_srcf, 1.0, None, ALU.add))
                v.scalar_tensor_tensor(out=e_key, in0=e_typef, scalar=float(P), in1=e_loc, op0=ALU.mult, op1=ALU.add)
                v.scalar_tensor_tensor(out=e_bucket, in0=e_tile, scalar=float(R), in1=e_typef,
                                       op0=ALU.mult, op1=ALU.add)
                link(v.memset(e_pos, -1.0))
                link(v.tensor_scalar(e_key, e_key, 1.0, None, ALU.add))
                for t in range(TILES):
                    i = v.tensor_scalar(e_mask, e_tile, float(t), 0.0, ALU.is_equal, ALU.add,
                                        accum_out=e_totals[:, t:t + 1])
                    link(i)
                v.wait_ge(iota_done, 1)
                v.tensor_copy(iota_f, iota_i)
                link(v.tensor_copy(iota_h, iota_i))
                v.memset(e_scan, 0.0).then_inc(totals_done, 1)
                for q in range(4):
                    v.wait_ge(w_ready_hi, 4 + q + 1)
                    lo_piece(v, 1, 1, q)
                v.wait_ge(prefix_done, 1)
                v.tensor_copy(t_off, CNT_BANK[:, 0:TILES])
                link(v.tensor_copy(t_count, CNT_BANK[:, TILES:2 * TILES]))
                link(v.tensor_scalar(t_count, t_count, float(GROUP * P - 1), None, ALU.add))
                link(v.tensor_copy(t_int, t_count))
                link(v.tensor_scalar(t_int, t_int, (GROUP * P).bit_length() - 1, None, ALU.logical_shift_right))
                link(v.tensor_copy(t_groups, t_int))
                link(v.memset(t_start, 0.0))
                for t in range(1, TILES):
                    link(v.tensor_tensor(t_start[:, t:t + 1], t_start[:, t - 1:t], t_groups[:, t - 1:t], ALU.add))
                link(v.scalar_tensor_tensor(out=t_off, in0=t_start, scalar=float(GROUP * P), in1=t_off,
                                            op0=ALU.mult, op1=ALU.add))
                link(v.tensor_scalar(t_start, t_start, float(GROUP), None, ALU.mult))
                for t in range(TILES):
                    link(v.tensor_scalar(e_mask, e_tile, float(t), None, ALU.is_equal))
                    link(v.tensor_tensor_scan(e_scan, e_ones, e_mask, 0.0, ALU.mult, ALU.add))
                    link(v.scalar_tensor_tensor(out=e_scan, in0=e_scan, scalar=t_off[:EP, t:t + 1], in1=e_mask,
                                                op0=ALU.add, op1=ALU.mult))
                    link(v.tensor_tensor(e_pos, e_pos, e_scan, ALU.add))
                link(v.tensor_copy(e_tile_i, e_pos))
                v.tensor_scalar(e_loc_i, e_tile_i, P - 1, None, ALU.bitwise_and)
                link(v.tensor_scalar(e_tile_i, e_tile_i, P.bit_length() - 1, None, ALU.logical_shift_right))
                v.tensor_copy(e_p, e_loc_i)
                link(v.tensor_copy(e_j, e_tile_i))

                def column(col, slot, wait):
                    if wait:
                        v.wait_ge(hot_used, col - 3)
                    at = bass.ds(col, 1)
                    v.tensor_scalar(hot_p[:, slot, :], iota_h[:EP, 0:P], e_p[:, at], None, ALU.is_equal)
                    v.tensor_scalar(hot_src[:, slot, :], iota_h[:EP, :], e_j[:, at], e_srcf[:, at],
                                    ALU.is_equal, ALU.mult)
                    v.tensor_scalar(hot_key[:, slot, :], iota_h[:EP, :], e_j[:, at], e_key[:, at],
                                    ALU.is_equal, ALU.mult)
                    v.tensor_scalar(hot_bucket[:, slot, :], iota_h[:EP, 0:BUCKETS], e_bucket[:, at], None, ALU.is_equal)
                    v.tensor_scalar(hot_local[:, slot, :], iota_h[:EP, 0:P], e_loc[:, at], None, ALU.is_equal)\
                        .then_inc(hot_ready, 1)

                def chunk(c, s, cols=None, first=False):
                    for m in range(TILES):
                        if cols is not None:
                            for q in range(COLS_PER_TILE):
                                column(cols + m * COLS_PER_TILE + q, q, not (first and m == 0))
                        if m in (1, 3, 5, 7):
                            lo_piece(v, c + 1, 1 - s, (m - 1) // 2)

                chunk(1, 1)
                step = TILES * COLS_PER_TILE
                for s in range(2):
                    chunk(2 + s, s, cols=s * step, first=(s == 0))
                with v.Fori(1, INDEX_CHUNKS // 2) as i:
                    for s in range(2):
                        chunk(2 * i + 2 + s, s, cols=i * (2 * step) + s * step)

                v.wait_ge(hot_used, EC)
                link(v.memset(l_recip[:, :], 0.0))
                link(v.tensor_scalar(l_recip[:BUCKETS, :], CNT_BANK[:BUCKETS, 0:P], 1.0, None, ALU.max))
                v.reciprocal(l_recip[:BUCKETS, :], l_recip[:BUCKETS, :]).then_inc(recip_made, 1)
                link(v.tensor_scalar(l_key, KEY_BANK[:, 0:BLOCKS], -1.0, None, ALU.add))
                link(v.tensor_copy(l_keyi, l_key))
                v.tensor_scalar(l_reli, l_keyi, P.bit_length() - 1, None, ALU.arith_shift_right)
                link(v.tensor_scalar(l_loci, l_keyi, P - 1, None, ALU.bitwise_and))
                v.tensor_copy(sort_local[:, :], l_loci)
                link(v.tensor_copy(l_relf, l_reli))
                link(v.scalar_tensor_tensor(out=l_row, in0=l_relf, scalar=float(N), in1=SRC_BANK[:, 0:BLOCKS],
                                            op0=ALU.mult, op1=ALU.add))
                link(v.tensor_scalar(l_pad, l_key, 0.0, float(Y_PAD), ALU.is_lt, ALU.mult))
                link(v.scalar_tensor_tensor(out=l_row, in0=l_row, scalar=-1.0, in1=l_pad, op0=ALU.add, op1=ALU.add))
                v.tensor_copy(sort_row[:, :], l_row)
                link(v.memset(l_tile, 0.0))
                for t in range(1, TILES):
                    link(v.scalar_tensor_tensor(out=l_tile, in0=iota_f, scalar=t_start[:, t:t + 1], in1=l_tile,
                                                op0=ALU.is_ge, op1=ALU.add))
                v.tensor_copy(group_tile[:, :], l_tile.rearrange("p (g b) -> p g b", b=GROUP)[:, :, 0])
                link(v.scalar_tensor_tensor(out=l_at, in0=l_tile, scalar=float(R * P), in1=l_key,
                                            op0=ALU.mult, op1=ALU.add))
                link(v.tensor_scalar(l_pad, l_key, 0.0, None, ALU.is_ge))
                link(v.scalar_tensor_tensor(out=l_at, in0=l_at, scalar=-float(BUCKETS * P), in1=l_pad,
                                            op0=ALU.add, op1=ALU.mult))
                link(v.tensor_scalar(l_at, l_at, float(BUCKETS * P), None, ALU.add))
                v.tensor_copy(recip_at[:, :], l_at).then_inc(index_ready, 1)

                with v.Fori(INDEX_CHUNKS // 2 + 1, R) as i:
                    for s in range(2):
                        chunk(2 * i + s, s)
                v.wait_ge(bias_in, 32)
                v.wait_ge(recip_stored, 16)
                link(v.memset(acc[:, TILES - 1, :], 0.0))
                for s in range(4):
                    c = CH_ROOT + s
                    for m in range(TILES):
                        t, h = TILES * (s % 2) + m, s % 2
                        v.wait_ge(mm_done, c * TILES + m + 1)
                        if s < 2:
                            v.tensor_tensor(acc[:rows(m), m, h * HALF:(h + 1) * HALF], bank[t % 4][:rows(m), :],
                                            bias_bc[:rows(m), h * HALF:(h + 1) * HALF], ALU.add).then_inc(evac_v, 1)
                        else:
                            v.wait_ge(y_stored[t % 4], 16 * 5 * R + 16 * (t // 4))
                            v.tensor_tensor(stage_y[:rows(m), t % 4, :], bank[t % 4][:rows(m), :],
                                            gate_bc[:rows(m), h * HALF:(h + 1) * HALF], ALU.add).then_inc(evac_v, 1)
                        if m in (1, 3, 5, 7) and s < 3:
                            lo_piece(v, c + 1, 1 - s % 2, (m - 1) // 2)

            @block.gpsimd
            def _(pool):
                pool.memset(tri, 1.0).then_inc(pool_ch, 1)
                pool.memset(ones, 1.0).then_inc(pool_ch, 1)
                pool.memset(gate_word[:, :], 0.0).then_inc(pool_ch, 1)
                pool.wait_ge(pool_ch, 3)
                pool.affine_select(out=tri, in_=tri, compare_op=ALU.is_gt, fill=0.0, base=0,
                                   pattern=[[1, P]], channel_multiplier=-1).then_inc(pool_ch, 1)
                pool.iota(iota_i, pattern=[[1, BLOCKS]], base=0, channel_multiplier=0).then_inc(iota_done, 1)
                pool.wait_ge(recip_made, 1)
                pool.dma_start(recip_dram.rearrange("(b p) o -> b (p o)", p=P), l_recip[:BUCKETS + 1, :])\
                    .then_inc(recip_stored, 16)
                pool.wait_ge(recip_stored, 16)
                pool.wait_ge(index_ready, 1)
                pool.wait_ge(pool_ch, 4)
                with pool.Fori(0, BLOCKS // 8) as i:
                    pool.tensor_copy(l_slot_i[:, :], recip_at[:, bass.ds(i * 8, 8)]).then_inc(pool_ch, 1)
                    pool.wait_ge(pool_ch, 2 * i + 5)
                    pool.tensor_tensor(gate_word[:, 1:2], gate_word[:, 0:1], gate_word[:, 0:1], ALU.add)
                    for q in range(8):
                        pool.indirect_dma_start(l_slot_r[:, q:q + 1], None, recip_dram,
                                                IndirectOffsetOnAxis(ap=l_slot_i[:, q:q + 1], axis=0))\
                            .then_inc(rg[q], 16)
                    for q in range(8):
                        pool.wait_ge(rg[q], 16 * i + 16)
                    pool.tensor_copy(sort_recip[:, bass.ds(i * 8, 8)], l_slot_r[:, :]).then_inc(pool_ch, 1)
                    pool.wait_ge(pool_ch, 2 * i + 6)

        operands.close()

        SLOTS = 2 * GROUP
        DIRECT = GROUP - 1
        with ExitStack() as stage:
            def ssem(name):
                return stage.enter_context(nc.semaphore(name))

            def ssb(name, shape, dt=F32):
                return stage.enter_context(nc.sbuf_tensor(name, shape, dt))

            y_in = ssb("y_in", [P, SLOTS, D])
            hot = ssb("hot", [P, SLOTS, P], F32R)
            hot_scaled = ssb("hot_scaled", [P, 2, P])
            lanes = ssb("lanes", [P, P])
            lanes_i = ssb("lanes_i", [P, P], I32)
            row_s, recip_s, local_s = ssb("row_s", [P, SLOTS], I32), ssb("recip_s", [P, SLOTS]), ssb("local_s", [P, SLOTS])
            y_hi = w_hi[:, :, :].rearrange("p s (q n) -> p (s q) n", n=D)
            y_lo = w_lo[:, :, :].rearrange("p s (q n) -> p (s q) n", n=D)

            got = [ssem(f"g_got{b}") for b in range(SLOTS)]
            used_hi = [ssem(f"g_usedhi{b}") for b in range(SLOTS)]
            used_v = [ssem(f"g_usedv{b}") for b in range(SLOTS)]
            used_pe = [ssem(f"g_usedpe{b}") for b in range(SLOTS)]
            cleared, lanes_done, copied = ssem("g_clear"), ssem("g_lanes"), ssem("g_copied")
            vch = ssem("g_vch")
            flushed = [ssem("g_flush0"), ssem("g_flush1")]
            block = stage.enter_context(nc.Block())

            @block.gpsimd
            def _(pool):
                pool.iota(lanes_i[:, :], pattern=[[1, P]], base=0, channel_multiplier=0).then_inc(lanes_done, 1)
                for b in range(SLOTS):
                    pool.memset(y_in[:, b, :], 0.0).then_inc(cleared, 1)
                pool.wait_ge(cleared, SLOTS)
                def pair(i):
                    for h in range(2):
                        part = slice(h * GROUP, (h + 1) * GROUP)
                        for b in range(h * GROUP, (h + 1) * GROUP):
                            wait_after_first(pool, got[b], 16 * i)
                            wait_after_first(pool, used_v[b], i)
                            if b % GROUP == DIRECT:
                                wait_after_first(pool, used_pe[b], i)
                            else:
                                wait_after_first(pool, used_hi[b], i)
                        at = bass.ds(i * SLOTS + h * GROUP, GROUP)
                        pool.tensor_copy(recip_s[:, part], sort_recip[:, at]).then_inc(copied, 1)
                        pool.tensor_copy(local_s[:, part], sort_local[:, at]).then_inc(copied, 1)
                        pool.tensor_copy(row_s[:, part], sort_row[:, at]).then_inc(copied, 1)
                        pool.wait_ge(copied, 6 * i + 3 * h + 3)
                        pool.tensor_tensor(gate_word[:, 1:2], gate_word[:, 0:1], gate_word[:, 0:1], ALU.add)
                        for b in range(h * GROUP, (h + 1) * GROUP):
                            pool.indirect_dma_start(y_in[:, b, :], None, y_dram,
                                                    IndirectOffsetOnAxis(ap=row_s[:, b:b + 1], axis=0),
                                                    bounds_check=R * N - 1, oob_is_err=False)\
                                .then_inc(got[b], 16)

                pair(0)
                with pool.Fori(1, GROUPS // 2) as i:
                    pair(i)

            @block.scalar
            def _(act):
                def pair(i):
                    for b in range(SLOTS):
                        if b % GROUP == DIRECT:
                            continue
                        act.wait_ge(got[b], 16 * i + 16)
                        act.wait_ge(copied, 6 * i + 3 * (b // GROUP) + 3)
                        wait_after_first(act, used_pe[b], i)
                        act.activation(y_hi[:, b, :], y_in[:, b, :], ACT.Copy, scale=recip_s[:, b:b + 1])\
                            .then_inc(used_hi[b], 1)

                pair(0)
                with act.Fori(1, GROUPS // 2) as i:
                    pair(i)

            @block.vector
            def _(v):
                v.wait_ge(lanes_done, 1)
                v.tensor_copy(lanes[:, :], lanes_i[:, :]).then_inc(vch, 1)
                v.wait_ge(vch, 1)

                def blocks(i, h):
                    for b in range(h * GROUP, (h + 1) * GROUP):
                        v.wait_ge(copied, 6 * i + 3 * h + 3)
                        wait_after_first(v, used_pe[b], i)
                        if b % GROUP == DIRECT:
                            v.tensor_scalar(hot_scaled[:, h, :], lanes[:, :], local_s[:, b:b + 1], recip_s[:, b:b + 1],
                                            ALU.is_equal, ALU.mult).then_inc(used_v[b], 1)
                        else:
                            v.tensor_scalar(hot[:, b, :], lanes[:, :], local_s[:, b:b + 1], None, ALU.is_equal)
                            v.wait_ge(used_hi[b], i + 1)
                            v.scalar_tensor_tensor(out=y_lo[:, b, :], in0=y_in[:, b, :], scalar=recip_s[:, b:b + 1],
                                                   in1=y_hi[:, b, :].bitcast(F32), op0=ALU.mult, op1=ALU.subtract)\
                                .then_inc(used_v[b], 1)

                def flush(g, h, passes):
                    v.wait_ge(used_pe[(h + 1) * GROUP - 1], passes)
                    tile = v.value_load(group_tile[0:1, bass.ds(g, 1)], min_val=0, max_val=TILES - 1)
                    for q in range(2):
                        u = acc[:, bass.ds(tile, 1), q * HALF:(q + 1) * HALF].rearrange("p o n -> p (o n)")
                        last = v.tensor_tensor(u, u, bank[2 * h + q][:, :], ALU.add)
                    last.then_inc(flushed[h], 1)
                    v.wait_ge(flushed[h], passes)

                blocks(0, 0)
                blocks(0, 1)
                flush(0, 0, 1)
                with v.Fori(1, GROUPS // 2) as i:
                    blocks(i, 0)
                    flush(2 * i - 1, 1, i)
                    blocks(i, 1)
                    flush(2 * i, 0, i + 1)
                flush(GROUPS - 1, 1, GROUPS // 2)

            @block.tensor
            def _(pe):
                def pair(i):
                    for h in range(2):
                        wait_after_first(pe, flushed[h], i)
                        for b in range(h * GROUP, (h + 1) * GROUP):
                            pe.wait_ge(used_v[b], i + 1)
                            first, last = b % GROUP == 0, b % GROUP == GROUP - 1
                            if b % GROUP == DIRECT:
                                pe.wait_ge(got[b], 16 * i + 16)
                                for q in range(2):
                                    m = pe.matmul(bank[2 * h + q][:, :], hot_scaled[:, h, :],
                                                  y_in[:, b, q * HALF:(q + 1) * HALF], start=first, stop=last)
                            else:
                                for y in (y_hi, y_lo):
                                    for q in range(2):
                                        m = pe.matmul(bank[2 * h + q][:, :], hot[:, b, :],
                                                      y[:, b, q * HALF:(q + 1) * HALF],
                                                      start=first and y is y_hi, stop=False)
                            m.then_inc(used_pe[b], 1)

                pair(0)
                with pe.Fori(1, GROUPS // 2) as i:
                    pair(i)
        sorting.close()

        opT_hi = sb("opT_hi", [P, KD, N], F32R)
        opT_lo = sb("opT_lo", [P, KD, N], F32R)
        with ExitStack() as stage:
            def ssem(name):
                return stage.enter_context(nc.semaphore(name))

            def ssb(name, shape, dt=F32):
                return stage.enter_context(nc.sbuf_tensor(name, shape, dt))

            x_s = ssb("x_s", [P, 2, D])
            z_s = ssb("z_s", [P, 2, D])
            th = w_raw

            x_in, zx_in = [ssem("z_x0"), ssem("z_x1")], [ssem("z_zx0"), ssem("z_zx1")]
            raw_in, raw_hi, raw_lo = [ssem("z_raw0"), ssem("z_raw1")], ssem("z_rawhi"), ssem("z_rawlo")
            wr_in, wr_done = ssem("z_wr"), ssem("z_wrdone")
            uT_done, uhi, ulo = ssem("z_uT"), ssem("z_uhi"), ssem("z_ulo")
            tT_done, thi, tlo = ssem("z_tT"), ssem("z_thi"), ssem("z_tlo")
            tanh_done, z_done, z_read = ssem("z_tanh"), ssem("z_z"), ssem("z_zread")
            var_ready, std_ready = ssem("z_var"), ssem("z_std")
            x1_ready, t_ready, lg_done, lg_out = ssem("z_x1r"), ssem("z_t"), ssem("z_lg"), ssem("z_lgout")
            x1_stored = [ssem("z_st0"), ssem("z_st1")]
            vch, th_free = ssem("z_vch"), ssem("z_thfree")
            block = stage.enter_context(nc.Block())
            NPW = 2 * PIECES

            def load_rows(sp, m):
                at = slice(m * P, m * P + rows(m))
                sp.dma_start(x_s[:rows(m), m % 2, :], x[at, :]).then_inc(x_in[m % 2], 16)
                sp.dma_start(z_s[:rows(m), m % 2, :], zx_dram[at, :]).then_inc(zx_in[m % 2], 16)

            def store_rows(sp, m):
                sp.wait_ge(t_ready, m + 1)
                sp.dma_start(x1_dram[m * P:m * P + rows(m), :], x_s[:rows(m), m % 2, :]).then_inc(x1_stored[m % 2], 16)

            @block.sync
            def _(sp):
                for i in range(NPW):
                    if i >= 2:
                        sp.wait_ge(raw_hi, i - 1)
                        sp.wait_ge(raw_lo, i - 1)
                    c, q = CH_GATEU + i // PIECES, i % PIECES
                    sp.dma_start(w_raw[:, i % 2, :], wchunks[c * P:(c + 1) * P, q * PIECE:(q + 1) * PIECE])\
                        .then_inc(raw_in[i % 2], 16)
                    if i == 0:
                        sp.dma_start(wr_raw[:, :, :], wr).then_inc(wr_in, 16)
                        sp.dma_start(br_bc[:, :], br[0:1, :].to_broadcast([P, E])).then_inc(wr_in, 16)
                        sp.dma_start(b1_sb[:, :, :], b1).then_inc(wr_in, 16)
                    if i in (1, 2):
                        load_rows(sp, i - 1)
                for m in range(2, TILES):
                    store_rows(sp, m - 2)
                    sp.wait_ge(x1_stored[m % 2], 16 * (m // 2))
                    load_rows(sp, m)
                store_rows(sp, TILES - 2)
                store_rows(sp, TILES - 1)
                for i in range(2):
                    sp.wait_ge(x1_stored[i], 16 * (TILES // 2))

            def four(b, rm):
                return bank[b][:, :].rearrange("p (k n) -> p k n", k=4)[:, :, :rm]

            @block.scalar
            def _(act):
                for i in range(NPW):
                    act.wait_ge(raw_in[i % 2], 16 * (i // 2 + 1))
                    act.activation(w_hi[:, i // PIECES, (i % PIECES) * PIECE:(i % PIECES + 1) * PIECE],
                                   w_raw[:, i % 2, :], ACT.Copy).then_inc(raw_hi, 1)
                act.wait_ge(wr_in, 48)
                act.activation(wr_hi[:, :, :], wr_raw[:, :, :], ACT.Copy).then_inc(wr_done, 1)

                def hi(m, done, out_sem, b):
                    act.wait_ge(done, m + 1)
                    for q in range(2):
                        act.activation(opT_hi[:, 4 * q:4 * q + 4, m * P:m * P + rows(m)], four(b + q, rows(m)), ACT.Copy)\
                            .then_inc(out_sem, 1)

                for s in range(-1, TILES + 2):
                    if s + 1 < TILES:
                        hi(s + 1, uT_done, uhi, 4)
                    if 0 <= s < TILES:
                        if s >= 2:
                            act.wait_ge(x1_ready, s - 1)
                        act.wait_ge(raw_lo, NPW)
                        act.activation(th[:rows(s), s % 2, :], acc[:rows(s), s, :], ACT.Tanh).then_inc(tanh_done, 1)
                    if 0 <= s - 1 < TILES:
                        hi(s - 1, tT_done, thi, 6)
                    if 0 <= s - 2 < TILES:
                        act.wait_ge(lg_done, s - 1)
                        act.activation(router[:rows(s - 2), s - 2, :], bank[4][:rows(s - 2), 0:E], ACT.Copy)\
                            .then_inc(lg_out, 1)
                    if 0 <= s < TILES:
                        act.wait_ge(var_ready, s + 1)
                        act.activation(rs[:rows(s), s % 2, 1:2], rs[:rows(s), s % 2, 0:1], ACT.Sqrt)\
                            .then_inc(std_ready, 1)

            @block.tensor
            def _(pe):
                def transposed(m, b, done):
                    for k in range(KD):
                        t = pe.transpose(bank[b + k // 4][:, (k % 4) * P:(k % 4) * P + rows(m)],
                                         acc[:rows(m), m, k * P:(k + 1) * P], ident[:rows(m), :rows(m)])
                    t.then_inc(done, 1)

                for s in range(-1, TILES + 2):
                    if s + 1 < TILES:
                        if s >= 0:
                            pe.wait_ge(ulo, 2 * (s + 1))
                        if s - 3 >= 0:
                            pe.wait_ge(lg_out, s - 2)
                        transposed(s + 1, 4, uT_done)
                    if 0 <= s < TILES:
                        pe.wait_ge(uhi, 2 * s + 2)
                        pe.wait_ge(ulo, 2 * s + 2)
                        if s >= 2:
                            pe.wait_ge(z_read, s - 1)
                        rm, b = rows(s), 2 * (s % 2)
                        for q in range(2):
                            if s == 0:
                                pe.wait_ge(raw_hi, PIECES * (q + 1))
                                pe.wait_ge(raw_lo, PIECES * (q + 1))
                            n = 0
                            for a_, b_ in ((opT_hi, w_hi), (opT_hi, w_lo), (opT_lo, w_hi)):
                                for k in range(KD):
                                    i = pe.matmul(bank[b + q][:rm, :], a_[:, k, s * P:s * P + rm],
                                                  b_[:, q, k * HALF:(k + 1) * HALF],
                                                  start=(n == 0), stop=(n == 3 * KD - 1))
                                    n += 1
                        i.then_inc(z_done, 1)
                    if 0 <= s - 1 < TILES:
                        pe.wait_ge(t_ready, s)
                        if s - 2 >= 0:
                            pe.wait_ge(tlo, 2 * (s - 1))
                        transposed(s - 1, 6, tT_done)
                    if 0 <= s - 2 < TILES:
                        m = s - 2
                        pe.wait_ge(ulo, 2 * min(s + 2, TILES))
                        pe.wait_ge(thi, 2 * m + 2)
                        pe.wait_ge(tlo, 2 * m + 2)
                        pe.wait_ge(wr_done, 2)
                        if m >= 1:
                            pe.wait_ge(lg_out, m)
                        n = 0
                        for a_, b_ in ((opT_hi, wr_hi), (opT_hi, wr_lo), (opT_lo, wr_hi)):
                            for k in range(KD):
                                i = pe.matmul(bank[4][:rows(m), 0:E], a_[:, k, m * P:m * P + rows(m)], b_[:, k, :],
                                              start=(n == 0), stop=(n == 3 * KD - 1))
                                n += 1
                        i.then_inc(lg_done, 1)

            @block.vector
            def _(v):
                n = [0]

                def link(ins):
                    n[0] += 1
                    ins.then_inc(vch, 1)
                    v.wait_ge(vch, n[0])

                for i in range(NPW):
                    v.wait_ge(raw_hi, i + 1)
                    at = slice((i % PIECES) * PIECE, (i % PIECES + 1) * PIECE)
                    v.tensor_tensor(w_lo[:, i // PIECES, at], w_raw[:, i % 2, :], w_hi[:, i // PIECES, at].bitcast(F32),
                                    ALU.subtract).then_inc(raw_lo, 1)
                v.memset(router[:, :, :], 0.0).then_inc(vch, 1)
                n[0] += 1
                v.wait_ge(wr_done, 1)
                v.tensor_tensor(wr_lo[:, :, :], wr_raw[:, :, :], wr_hi[:, :, :].bitcast(F32), ALU.subtract)\
                    .then_inc(wr_done, 1)

                def lo(m, hi_sem, out_sem, b):
                    for q in range(2):
                        v.wait_ge(hi_sem, 2 * m + q + 1)
                        cols = slice(m * P, m * P + rows(m))
                        v.tensor_tensor(opT_lo[:, 4 * q:4 * q + 4, cols], four(b + q, rows(m)),
                                        opT_hi[:, 4 * q:4 * q + 4, cols].bitcast(F32), ALU.subtract)\
                            .then_inc(out_sem, 1)

                for s in range(-1, TILES + 1):
                    if s + 1 < TILES:
                        lo(s + 1, uhi, ulo, 4)
                    if 0 <= s < TILES:
                        rm, a = rows(s), s % 2
                        xs, zs, ts, u = x_s[:rm, a, :], z_s[:rm, a, :], th[:rm, a, :], acc[:rm, s, :]
                        v.wait_ge(x_in[a], 16 * (s // 2 + 1))
                        v.wait_ge(tanh_done, s + 1)
                        v.wait_ge(uT_done, s + 1)
                        link(v.tensor_scalar(u, xs, mean_all[:rm, s:s + 1], rstd_all[:rm, s:s + 1],
                                             ALU.subtract, ALU.mult))
                        v.tensor_tensor(ts, ts, u, ALU.subtract)
                        link(v.tensor_tensor(xs, xs, u, ALU.add))
                        v.wait_ge(zx_in[a], 16 * (s // 2 + 1))
                        v.wait_ge(z_done, s + 1)
                        for q in range(2):
                            i = v.tensor_tensor(zs[:, q * HALF:(q + 1) * HALF], zs[:, q * HALF:(q + 1) * HALF],
                                                bank[2 * a + q][:rm, :], ALU.add)
                        i.then_inc(z_read, 1)
                        v.wait_ge(z_read, s + 1)
                        link(v.tensor_tensor(ts, ts, zs, ALU.mult))
                        v.tensor_tensor(xs, xs, ts, ALU.add).then_inc(x1_ready, 1)
                        v.wait_ge(x1_ready, s + 1)
                        norm_stats(v, link, xs, a, rm, var_ready)
                        v.wait_ge(std_ready, s + 1)
                        rstd(v, link, a, rm, rs[:rm, a, 3:4])
                        v.tensor_scalar(u, xs, aggr[:rm, a, 0:1], rs[:rm, a, 3:4], ALU.subtract, ALU.mult)\
                            .then_inc(t_ready, 1)
                    if 0 <= s - 1 < TILES:
                        lo(s - 1, thi, tlo, 6)

        with ExitStack() as stage:
            def ssem(name):
                return stage.enter_context(nc.semaphore(name))

            def ssb(name, shape, dt=F32):
                return stage.enter_context(nc.sbuf_tensor(name, shape, dt))

            hT_hi, hT_lo = ssb("hT_hi", [P, KF, HALF], F32R), ssb("hT_lo", [P, KF, HALF], F32R)
            h_s = ssb("h_s", [P, 1, HALF])
            raw_in, raw_hi, raw_lo = [ssem("e_raw0"), ssem("e_raw1")], ssem("e_rawhi"), ssem("e_rawlo")
            h_done, o_done, o_read = ssem("e_h"), ssem("e_o"), ssem("e_oread")
            h_out, h_hi, h_lo, router_exp, router_max, router_ready = (
                ssem("e_hout"), ssem("e_hhi"), ssem("e_hlo"), ssem("e_rexp"), ssem("e_rmax"), ssem("e_rready"))
            vch = ssem("e_vch")
            rk = ssb("rk", [P, 3, E])
            rk1 = ssb("rk1", [P, 4])
            block = stage.enter_context(nc.Block())
            ORDER = [(8, 10), (0, 4), (4, 8)]
            NP1, NT = KF * len(ORDER), TILES

            @block.sync
            def _(sp):
                def pieces(e):
                    for q in range(2 * PIECES):
                        wait_after_first(sp, raw_hi, 2 * PIECES * e + q - 1)
                        wait_after_first(sp, raw_lo, 2 * PIECES * e + q - 1)
                        sp.dma_start(w_raw[:, q % 2, :],
                                     wchunks[bass.ds(e * (2 * P) + (CH_EXP + q // PIECES) * P, P),
                                             (q % PIECES) * PIECE:(q % PIECES + 1) * PIECE]).then_inc(raw_in[q % 2], 16)

                pieces(0)
                with sp.Fori(1, E) as e:
                    pieces(e)

            def w_hi_piece(act, e, q):
                act.wait_ge(raw_in[q % 2], 16 * PIECES * e + 16 * (q // 2 + 1))
                act.activation(w_hi[:, q // PIECES, (q % PIECES) * PIECE:(q % PIECES + 1) * PIECE],
                               w_raw[:, q % 2, :], ACT.Copy).then_inc(raw_hi, 1)

            def w_lo_piece(v, e, q):
                at = slice((q % PIECES) * PIECE, (q % PIECES + 1) * PIECE)
                v.wait_ge(raw_hi, 2 * PIECES * e + q + 1)
                v.tensor_tensor(w_lo[:, q // PIECES, at], w_raw[:, q % 2, :], w_hi[:, q // PIECES, at].bitcast(F32),
                                ALU.subtract).then_inc(raw_lo, 1)

            def width(t0, t1):
                return min(t1 * P, N) - t0 * P

            @block.scalar
            def _(act):
                for m in range(TILES):
                    act.wait_ge(router_max, m + 1)
                    act.activation(rk[:rows(m), 2, :], router[:rows(m), m, :], ACT.Exp, bias=rk1[:rows(m), 1:2])\
                        .then_inc(router_exp, 1)
                for q in range(2 * PIECES):
                    w_hi_piece(act, 0, q)

                def expert(e, last=False):
                    for j, (t0, t1) in enumerate(ORDER):
                        w = width(t0, t1)
                        for f in range(KF):
                            g = j * KF + f
                            act.wait_ge(h_done, NP1 * e + g + 1)
                            wait_after_first(act, h_lo, NP1 * e + g)
                            b1_col = b1_here[:, f:f + 1]
                            act.activation(h_s[:, 0, :w], bank[f][:, :w], ACT.Relu, bias=b1_col).then_inc(h_out, 1)
                            act.wait_ge(h_out, NP1 * e + g + 1)
                            act.activation(hT_hi[:, f, :w], h_s[:, 0, :w], ACT.Copy).then_inc(h_hi, 1)
                    if not last:
                        for q in range(PIECES):
                            w_hi_piece(act, e + 1, q)
                        act.wait_ge(o_done, 2 * NT * (e + 1))
                        for q in range(PIECES, 2 * PIECES):
                            w_hi_piece(act, e + 1, q)

                def bias_of(e):
                    act.activation(b1_here[:, :], b1_sb[:, bass.ds(e, 1), :].rearrange("p o f -> p (o f)"), ACT.Copy)\
                        .then_inc(b1_copied, 1)
                    act.wait_ge(b1_copied, e + 1)

                bias_of(0)
                expert(0)
                with act.Fori(1, E - 1) as e:
                    bias_of(e)
                    expert(e)
                bias_of(E - 1)
                expert(E - 1, last=True)

            @block.tensor
            def _(pe):
                def expert(e, first=False):
                    done = 0
                    for j, (t0, t1) in enumerate(ORDER):
                        w = width(t0, t1)
                        for f in range(KF):
                            if j == 0 and f == 0:
                                pe.wait_ge(raw_hi, 2 * PIECES * e + PIECES)
                                pe.wait_ge(raw_lo, 2 * PIECES * e + PIECES)
                            pe.wait_ge(h_out, NP1 * e + j * KF + f - 3) if not (first and j == 0) else None
                            n = 0
                            for a_, b_ in ((w_hi, opT_hi), (w_lo, opT_hi), (w_hi, opT_lo)):
                                for k in range(KD):
                                    i = pe.matmul(bank[f][:, :w], a_[:, 0, k * F + f * P:k * F + (f + 1) * P],
                                                  b_[:, k, t0 * P:t0 * P + w], start=(n == 0), stop=(n == 3 * KD - 1))
                                    n += 1
                            i.then_inc(h_done, 1)
                        if j == 0:
                            pe.wait_ge(raw_hi, 2 * PIECES * (e + 1))
                            pe.wait_ge(raw_lo, 2 * PIECES * (e + 1))
                        for m in range(t0, t1):
                            rm, at = rows(m), (m - t0) * P
                            for q in range(2):
                                b = 4 + (done % 4)
                                if not (first and done < 4):
                                    pe.wait_ge(o_read, 2 * NT * e + done - 3)
                                n = 0
                                for k in range(KF):
                                    if m == t0 and q == 0:
                                        pe.wait_ge(h_lo, NP1 * e + j * KF + k + 1)
                                    for a_, b_ in ((hT_hi, w_hi), (hT_hi, w_lo), (hT_lo, w_hi)):
                                        i = pe.matmul(bank[b][:rm, :], a_[:, k, at:at + rm],
                                                      b_[:, 1, k * D + q * HALF:k * D + (q + 1) * HALF],
                                                      start=(n == 0), stop=(n == 3 * KF - 1))
                                        n += 1
                                i.then_inc(o_done, 1)
                                done += 1

                expert(0, first=True)
                with pe.Fori(1, E) as e:
                    expert(e)

            @block.vector
            def _(v):
                n = [0]

                def link(ins):
                    n[0] += 1
                    ins.then_inc(vch, 1)
                    v.wait_ge(vch, n[0])

                for m in range(TILES):
                    rm = rows(m)
                    lg = router[:rm, m, :]
                    link(v.tensor_tensor(lg, lg, br_bc[:rm, :], ALU.add))
                    link(v.reduce_max(rk1[:rm, 0:1], lg, axis=AX.X))
                    v.tensor_scalar(rk1[:rm, 1:2], rk1[:rm, 0:1], -1.0, None, ALU.mult).then_inc(router_max, 1)
                    for e in range(E):
                        link(v.tensor_scalar(rk[:rm, 1, :], lg, lg[:, e:e + 1], 0.0, ALU.is_gt, ALU.add,
                                             accum_out=rk[:rm, 0, e:e + 1]))
                        if e:
                            link(v.tensor_scalar(rk[:rm, 1, 0:e], lg[:, 0:e], lg[:, e:e + 1], 0.0, ALU.is_equal, ALU.add,
                                                 accum_out=rk1[:rm, 2:3]))
                            link(v.tensor_tensor(rk[:rm, 0, e:e + 1], rk[:rm, 0, e:e + 1], rk1[:rm, 2:3], ALU.add))
                    v.wait_ge(router_exp, m + 1)
                    link(v.scalar_tensor_tensor(out=lg, in0=rk[:rm, 0, :], scalar=2.0, in1=rk[:rm, 2, :],
                                                op0=ALU.is_lt, op1=ALU.mult))
                    link(v.reduce_sum(rk1[:rm, 2:3], lg, axis=AX.X))
                    link(v.reciprocal(rk1[:rm, 3:4], rk1[:rm, 2:3]))
                    link(v.tensor_scalar(lg, lg, rk1[:rm, 3:4], None, ALU.mult))
                for q in range(2 * PIECES):
                    w_lo_piece(v, 0, q)

                def expert(e, last=False):
                    v.tensor_copy(w_here[:, :], router[:, :, bass.ds(e, 1)].rearrange("p m o -> p (m o)"))\
                        .then_inc(w_copied, 1)
                    v.wait_ge(w_copied, e + 1)
                    done = 0
                    for j, (t0, t1) in enumerate(ORDER):
                        w = width(t0, t1)
                        for f in range(KF):
                            v.wait_ge(h_hi, NP1 * e + j * KF + f + 1)
                            v.tensor_tensor(hT_lo[:, f, :w], h_s[:, 0, :w], hT_hi[:, f, :w].bitcast(F32), ALU.subtract)\
                                .then_inc(h_lo, 1)
                        for m in range(t0, t1):
                            rm = rows(m)
                            if j == 2 and not last:
                                w_lo_piece(v, e + 1, m - t0)
                            for q in range(2):
                                v.wait_ge(o_done, 2 * NT * e + done + 1)
                                o = acc[:rm, m, q * HALF:(q + 1) * HALF]
                                v.scalar_tensor_tensor(out=o, in0=bank[4 + done % 4][:rm, :], scalar=w_here[:rm, m:m + 1],
                                                       in1=o, op0=ALU.mult, op1=ALU.add).then_inc(o_read, 1)
                                done += 1
                    if not last:
                        for q in range(PIECES, 2 * PIECES):
                            w_lo_piece(v, e + 1, q)

                with v.Fori(0, E - 1) as e:
                    expert(e)
                expert(E - 1, last=True)

        with ExitStack() as stage:
            def ssem(name):
                return stage.enter_context(nc.semaphore(name))

            def ssb(name, shape, dt=F32):
                return stage.enter_context(nc.sbuf_tensor(name, shape, dt))

            rT = ssb("rT", [E, 2, P])
            fin = ssb("fin", [P, 3, D])
            const_in, x1_in = ssem("f_const"), [ssem("f_x0"), ssem("f_x1")]
            b2_in = ssem("f_b2")
            rT_done, rT_out, b2_done, b2_read = ssem("f_rT"), ssem("f_rTout"), ssem("f_b2d"), ssem("f_b2read")
            var_ready, std_ready, y_ready = ssem("f_var"), ssem("f_std"), ssem("f_y")
            stored, vch = ssem("f_stored"), ssem("f_vch")
            gamma_bc, beta_bc = w_raw[:, 0, :], w_raw[:, 1, :]
            x1_s, b2_sb = fin[:, 0:2, :], fin[:E, 2, :]
            block = stage.enter_context(nc.Block())

            @block.sync
            def _(sp):
                sp.dma_start(b2_sb, b2).then_inc(b2_in, 16)
                sp.dma_start(gamma_bc, gamma[0:1, :].to_broadcast([P, D])).then_inc(const_in, 16)
                sp.dma_start(beta_bc, beta[0:1, :].to_broadcast([P, D])).then_inc(const_in, 16)
                for m in range(TILES + 1):
                    if m < TILES:
                        if m >= 2:
                            sp.wait_ge(y_ready, m - 1)
                        sp.dma_start(x1_s[:rows(m), m % 2, :], x1_dram[m * P:m * P + rows(m), :]).then_inc(x1_in[m % 2], 16)
                    if m >= 1:
                        k = m - 1
                        sp.wait_ge(y_ready, k + 1)
                        sp.dma_start(out[k * P:k * P + rows(k), :], acc[:rows(k), k, :]).then_inc(stored, 16)
                sp.wait_ge(stored, 16 * TILES)

            @block.tensor
            def _(pe):
                for m in range(TILES + 1):
                    if m < TILES:
                        if m >= 2:
                            pe.wait_ge(rT_out, m - 1)
                        pe.transpose(bank[m % 2][:E, 0:rows(m)], router[:rows(m), m, :], ident[:rows(m), :rows(m)])\
                            .then_inc(rT_done, 1)
                    if m >= 1:
                        k = m - 1
                        pe.wait_ge(b2_in, 16)
                        pe.wait_ge(rT_out, k + 1)
                        if k >= 2:
                            pe.wait_ge(b2_read, k - 1)
                        for q in range(2):
                            i = pe.matmul(bank[2 + 2 * (k % 2) + q][:rows(k), :], rT[:, k % 2, :rows(k)],
                                          b2_sb[:, q * HALF:(q + 1) * HALF], start=True, stop=True)
                        i.then_inc(b2_done, 1)

            @block.scalar
            def _(act):
                for m in range(TILES + 1):
                    if m < TILES:
                        act.wait_ge(rT_done, m + 1)
                        if m >= 2:
                            act.wait_ge(b2_done, m - 1)
                        act.activation(rT[:, m % 2, :rows(m)], bank[m % 2][:E, 0:rows(m)], ACT.Copy).then_inc(rT_out, 1)
                    if m >= 1:
                        k, a = m - 1, (m - 1) % 2
                        act.wait_ge(var_ready, k + 1)
                        act.activation(rs[:rows(k), a, 1:2], rs[:rows(k), a, 0:1], ACT.Sqrt).then_inc(std_ready, 1)

            @block.vector
            def _(v):
                n = [0]

                def link(ins):
                    n[0] += 1
                    ins.then_inc(vch, 1)
                    v.wait_ge(vch, n[0])

                v.wait_ge(const_in, 32)
                for m in range(TILES):
                    rm, a = rows(m), m % 2
                    o = acc[:rm, m, :]
                    v.wait_ge(b2_done, m + 1)
                    for q in range(2):
                        i = v.tensor_tensor(o[:, q * HALF:(q + 1) * HALF], o[:, q * HALF:(q + 1) * HALF],
                                            bank[2 + 2 * a + q][:rm, :], ALU.add)
                    i.then_inc(b2_read, 1)
                    v.wait_ge(b2_read, m + 1)
                    norm_stats(v, link, o, a, rm, var_ready)
                    v.wait_ge(std_ready, m + 1)
                    rstd(v, link, a, rm, rs[:rm, a, 3:4])
                    link(v.tensor_scalar(o, o, aggr[:rm, a, 0:1], rs[:rm, a, 3:4], ALU.subtract, ALU.mult))
                    link(v.tensor_tensor(o, o, gamma_bc[:rm, :], ALU.mult))
                    link(v.tensor_tensor(o, o, beta_bc[:rm, :], ALU.add))
                    v.wait_ge(x1_in[a], 16 * (m // 2 + 1))
                    v.tensor_tensor(o, o, x1_s[:rm, a, :], ALU.add).then_inc(y_ready, 1)


_OUTS = [((N, D), "float32")]


def kernel(**inputs):
    import numpy as np
    import concourse.bacc as bacc
    from concourse.bass_utils import run_bass_kernel_spmd as run

    def a(name):
        return np.ascontiguousarray(np.asarray(inputs[name]))

    def halves(w):
        return [w[:, h * HALF:(h + 1) * HALF].reshape(-1, P, HALF).transpose(1, 0, 2).reshape(P, -1)
                for h in range(2)]

    weight, root, gate = a("L0_gnn_weight"), a("L0_gnn_root"), a("L0_gnn_w_gate")
    w1, w2 = a("L0_ffn_W1"), a("L0_ffn_W2")
    chunks = []
    for r in range(R):
        chunks += halves(weight[r])
    chunks += halves(root) + halves(gate[D:]) + halves(gate[:D])
    for e in range(E):
        chunks.append(w1[e].T.reshape(KD, P, F).transpose(1, 0, 2).reshape(P, -1))
        chunks.append(w2[e].T.reshape(KF, P, D).transpose(1, 0, 2).reshape(P, -1))
    arrays = {
        "x": a("x"),
        "src": a("src").reshape(EP, EC), "dst": a("dst").reshape(EP, EC),
        "etype": a("edge_type_8").reshape(EP, EC),
        "wchunks": np.concatenate(chunks),
        "bias": a("L0_gnn_bias").reshape(1, D), "b_gate": a("L0_gnn_b_gate").reshape(1, D),
        "wr": np.ascontiguousarray(a("L0_ffn_Wr").T.reshape(KD, P, E).transpose(1, 0, 2)),
        "br": a("L0_ffn_br").reshape(1, E),
        "b1": np.ascontiguousarray(a("L0_ffn_b1").reshape(E, KF, P).transpose(2, 0, 1)),
        "b2": a("L0_ffn_b2"),
        "gamma": a("L0_ffn_gamma").reshape(1, D), "beta": a("L0_ffn_beta").reshape(1, D),
    }
    nc = bacc.Bacc("TRN2", target_bir_lowering=False, num_devices=1, dynamic_dma_scratch_size=8192)
    args, feed = [], {}
    for name, v in arrays.items():
        feed[f"in_{name}"] = v
        args.append(nc.dram_tensor(f"in_{name}", v.shape, mybir.dt.from_np(v.dtype), kind="ExternalInput").ap())
    args.append(nc.dram_tensor("out_0", _OUTS[0][0], F32, kind="ExternalOutput").ap())
    program(nc, *args)
    r = run(nc, [feed], core_ids=[0])
    return r.results[0]["out_0"]
```

```python
from contextlib import ExitStack

import concourse.bass as bass
import concourse.mybir as mybir
from concourse.bass import IndirectOffsetOnAxis

F32 = mybir.dt.float32
F32R = mybir.dt.float32r
F16 = mybir.dt.float16
I32 = mybir.dt.int32
ALU = mybir.AluOpType
ACT = mybir.ActivationFunctionType
AX = mybir.AxisListType

P = 128
N, D, R, E, F = 1250, 1024, 8, 8, 512
HALF = 512
TILES = -(-N // P)
KD = D // P
KF = F // P
EDGES, EP = 40000, 125
EC = EDGES // EP
GROUP = 4
GROUPS = (EDGES + TILES * (GROUP * P - 1)) // (GROUP * P)
BLOCKS = GROUPS * GROUP
BLOCK_T = 2 * P
BLOCKS_T = (2 * N + E * (BLOCK_T - 1)) // BLOCK_T
TILES_T = 2 * BLOCKS_T
BUCKETS = TILES * R
CHUNKS_R, CH_ROOT, CH_GATEX, CH_GATEU, CH_EXP = 2 * R, 2 * R, 2 * R + 2, 2 * R + 4, 2 * R + 6
CW = KD * HALF
PIECE = 1024
PIECES = CW // PIECE
EPS = 1e-5
Y_PAD = 1 << 20
COLS_PER_TILE = 4
INDEX_CHUNKS = EC // (TILES * COLS_PER_TILE)


def rows(m):
    return min(P, N - m * P)


def program(nc, x, src, dst, etype, wchunks, bias, b_gate, wr, br, b1, b2, gamma, beta, out):
    ctx = ExitStack()
    with ctx:
        def sb(name, shape, dt=F32):
            return ctx.enter_context(nc.sbuf_tensor(name, shape, dt))

        def sem(name):
            return ctx.enter_context(nc.semaphore(name))

        y_dram = nc.dram_tensor("y_rows", (R * N, D), F32, kind="Internal").ap()
        zx_dram = nc.dram_tensor("zx_rows", (N, D), F32, kind="Internal").ap()
        x1_dram = nc.dram_tensor("x1_rows", (N, D), F32, kind="Internal").ap()
        t_dram = nc.dram_tensor("t_rows", (N, D), F32, kind="Internal").ap()
        o_dram = nc.dram_tensor("o_rows", (TILES_T * P, D), F32, kind="Internal").ap()
        recip_dram = nc.dram_tensor("recip_table", (BUCKETS * P + P, 1), F32, kind="Internal").ap()

        w_hi = sb("w_hi", [P, 2, CW], F32R)
        w_lo = sb("w_lo", [P, 2, CW], F32R)
        w_raw = sb("w_raw", [P, 2, PIECE])
        acc = sb("acc", [P, TILES, D])
        ident = sb("ident", [P, P])
        mean_all = sb("mean_all", [P, TILES])
        rstd_all = sb("rstd_all", [P, TILES])
        router = sb("router", [P, TILES, E])
        b1_sb = sb("b1_sb", [P, E, KF])
        wr_raw = sb("wr_raw", [P, KD, E])
        wr_hi = sb("wr_hi", [P, KD, E], F32R)
        wr_lo = sb("wr_lo", [P, KD, E], F32R)
        br_bc = sb("br_bc", [P, E])
        stats = sb("stats", [P, 2, 2, 6])
        aggr = sb("aggr", [P, 2, 2])
        rs = sb("rs", [P, 2, 4])
        b1_here = sb("b1_here", [P, KF])
        sorting = ctx.enter_context(ExitStack())

        def sort_sb(name, shape, dt=F32):
            return sorting.enter_context(nc.sbuf_tensor(name, shape, dt))

        sort_row = sort_sb("sort_row", [P, BLOCKS], I32)
        sort_local = sort_sb("sort_local", [P, BLOCKS])
        sort_recip = sort_sb("sort_recip", [P, BLOCKS])
        group_tile = sort_sb("group_tile", [P, GROUPS], I32)
        recip_at = sort_sb("recip_at", [P, BLOCKS], I32)
        gate_word = sort_sb("gate_word", [1, 2])
        l_slot_i, l_slot_r = sort_sb("l_slot_i", [P, 8], I32), sort_sb("l_slot_r", [P, 8])
        operands = ctx.enter_context(ExitStack())
        xnT_hi = operands.enter_context(nc.sbuf_tensor("xnT_hi", [P, KD, N], F32R))
        xnT_lo = operands.enter_context(nc.sbuf_tensor("xnT_lo", [P, KD, N], F32R))
        work = operands.enter_context(nc.sbuf_tensor("work", [P, 4096], F32))
        bank = [ctx.enter_context(nc.psum_tensor(f"bank{i}", [P, HALF], F32)) for i in range(8)]

        w_ready_hi, w_ready_lo = sem("w_ready_hi"), sem("w_ready_lo")
        w_loaded = [sem("w_loaded0"), sem("w_loaded1")]
        mm_done, evac_done, evac_v = sem("p_mm"), sem("p_evac"), sem("p_evac_v")
        y_stored = [sem(f"p_ystored{i}") for i in range(4)]
        b1_copied = sem("b1_copied")
        v_chain, v_links = sem("v_chain"), [0]

        def wait_after_first(eng, semaphore, count):
            if not isinstance(count, int) or count > 0:
                eng.wait_ge(semaphore, count)

        def chained(v):
            def link(ins):
                v_links[0] += 1
                ins.then_inc(v_chain, 1)
                v.wait_ge(v_chain, v_links[0])
            return link

        def transpose(pe, to, of, n=P):
            return pe.transpose(to, of, ident[:n, :n])

        def four(b, rm):
            return bank[b][:, :].rearrange("p (k n) -> p k n", k=4)[:, :, :rm]

        def norm_stats(v, link, of, a, rm, var_ready):
            for q in range(2):
                i = v.bn_stats(stats[:rm, a, q, :], of[:, q * HALF:(q + 1) * HALF])
            link(i)
            link(v.bn_aggr(aggr[:rm, a, :], stats[:rm, a, :, :]))
            v.tensor_scalar(rs[:rm, a, 0:1], aggr[:rm, a, 1:2], EPS, None, ALU.add).then_inc(var_ready, 1)

        def rstd(v, link, a, rm, to):
            s, root, r, w = (rs[:rm, a, k:k + 1] for k in range(4))
            link(v.reciprocal(r, root))
            link(v.tensor_tensor(w, r, r, ALU.mult))
            link(v.tensor_tensor(w, w, s, ALU.mult))
            link(v.tensor_scalar(w, w, -0.5, 1.5, ALU.mult, ALU.add))
            link(v.tensor_tensor(to, w, r, ALU.mult))

        def load_piece(sp, c, q):
            sp.dma_start(w_raw[:, q % 2, :], wchunks[bass.ds(c * P, P), q * PIECE:(q + 1) * PIECE])\
                .then_inc(w_loaded[q % 2], 16)

        def raw_free(sp, piece):
            sp.wait_ge(w_ready_hi, piece - 1)
            sp.wait_ge(w_ready_lo, piece - 1)

        def hi_piece(act, c, s, q):
            act.wait_ge(w_loaded[q % 2], 32 * c + 16 * (q // 2 + 1))
            act.activation(w_hi[:, s, q * PIECE:(q + 1) * PIECE], w_raw[:, q % 2, :], ACT.Copy)\
                .then_inc(w_ready_hi, 1)

        def lo_piece(v, c, s, q):
            v.wait_ge(w_ready_hi, 4 * c + q + 1)
            v.tensor_tensor(w_lo[:, s, q * PIECE:(q + 1) * PIECE], w_raw[:, q % 2, :],
                            w_hi[:, s, q * PIECE:(q + 1) * PIECE].bitcast(F32), ALU.subtract)\
                .then_inc(w_ready_lo, 1)

        def tile_products(pe, c, s, m):
            t, rm, n = TILES * s + m, rows(m), 0
            for x_, w_ in ((xnT_hi, w_hi), (xnT_hi, w_lo), (xnT_lo, w_hi)):
                for k in range(KD):
                    i = pe.matmul(bank[t % 4][:rm, :], x_[:, k, m * P:m * P + rm],
                                  w_[:, s, k * HALF:(k + 1) * HALF], start=(n == 0), stop=(n == 3 * KD - 1))
                    n += 1
            i.then_inc(mm_done, 1)

        stage_y = work[:, 0:4 * HALF].rearrange("p (s n) -> p s n", s=4)
        xa = acc[:, 0:4, :]
        xn = acc[:, 4:8, :]
        with ExitStack() as stage:
            x_loaded = [stage.enter_context(nc.semaphore(f"x_loaded{i}")) for i in range(4)]
            def ssem(name):
                return stage.enter_context(nc.semaphore(name))
            std_ready, var_ready, xn_ready, t_done, hi_done, lo_done = (
                ssem("n_std"), ssem("n_var"), ssem("n_xn"), ssem("n_t"), ssem("n_hi"), ssem("n_lo"))
            ident_cleared, ident_made = ssem("n_id0"), ssem("n_id1")
            block = stage.enter_context(nc.Block())

            @block.sync
            def _(sp):
                def load_x(m):
                    sp.dma_start(xa[:rows(m), m % 4, :], x[m * P:m * P + rows(m), :])\
                        .then_inc(x_loaded[m % 4], 16)

                load_x(0)
                load_piece(sp, 0, 0)
                load_x(1)
                load_piece(sp, 0, 1)
                load_x(2)
                for q in range(2, PIECES):
                    raw_free(sp, q)
                    load_piece(sp, 0, q)
                load_x(3)
                for m in range(TILES):
                    if m + 4 < TILES:
                        sp.wait_ge(xn_ready, m + 1)
                        load_x(m + 4)
                    if m < PIECES:
                        raw_free(sp, PIECES + m)
                        load_piece(sp, 1, m)
                    sp.wait_ge(evac_done, m + 1)
                    sp.dma_start(y_dram[m * P:m * P + rows(m), 0:HALF], stage_y[:rows(m), m % 4, :])\
                        .then_inc(y_stored[m % 4], 16)
                for q in range(2):
                    raw_free(sp, 2 * PIECES + q)
                    load_piece(sp, 2, q)

            @block.gpsimd
            def _(pool):
                pool.memset(ident[:, :], 0.0).then_inc(ident_cleared, 1)
                pool.wait_ge(ident_cleared, 1)
                pool.affine_select(out=ident[:, :], in_=ident[:, :], compare_op=ALU.not_equal, fill=1.0,
                                   base=0, pattern=[[-1, P]], channel_multiplier=1).then_inc(ident_made, 1)

            @block.vector
            def _(v):
                link = chained(v)

                def lo_parts(m):
                    for q in range(2):
                        v.wait_ge(hi_done, 2 * m + q + 1)
                        src_t = four(4 + 2 * (m % 2) + q, rows(m))
                        cols = slice(m * P, m * P + rows(m))
                        v.tensor_tensor(xnT_lo[:, 4 * q:4 * q + 4, cols], src_t,
                                        xnT_hi[:, 4 * q:4 * q + 4, cols].bitcast(F32), ALU.subtract)\
                            .then_inc(lo_done, 1)

                for m in range(TILES):
                    a, rm = m % 2, rows(m)
                    v.wait_ge(x_loaded[m % 4], 16 * (m // 4 + 1))
                    norm_stats(v, link, xa[:rm, m % 4, :], a, rm, var_ready)
                    link(v.tensor_copy(mean_all[:rm, m:m + 1], aggr[:rm, a, 0:1]))
                    v.wait_ge(std_ready, m + 1)
                    rstd(v, link, a, rm, rstd_all[:rm, m:m + 1])
                    if m >= 4:
                        v.wait_ge(t_done, m - 3)
                    v.tensor_scalar(xn[:rm, m % 4, :], xa[:rm, m % 4, :], mean_all[:rm, m:m + 1],
                                    rstd_all[:rm, m:m + 1], ALU.subtract, ALU.mult).then_inc(xn_ready, 1)
                    if m < 2:
                        for q in (2 * m, 2 * m + 1):
                            lo_piece(v, 0, 0, q)
                    if m >= 1:
                        lo_parts(m - 1)
                    if m in (2, 4, 6, 8):
                        lo_piece(v, 1, 1, m // 2 - 1)
                lo_parts(TILES - 1)

            @block.scalar
            def _(act):
                def hi_parts(m):
                    act.wait_ge(t_done, m + 1)
                    for q in range(2):
                        src_t = four(4 + 2 * (m % 2) + q, rows(m))
                        act.activation(xnT_hi[:, 4 * q:4 * q + 4, m * P:m * P + rows(m)], src_t, ACT.Copy)\
                            .then_inc(hi_done, 1)

                def evac(m):
                    act.wait_ge(mm_done, m + 1)
                    if m >= 4:
                        act.wait_ge(y_stored[m % 4], 16 * (m // 4))
                    act.activation(stage_y[:rows(m), m % 4, :], bank[m % 4][:rows(m), :], ACT.Copy)\
                        .then_inc(evac_done, 1)

                for m in range(TILES):
                    a, rm = m % 2, rows(m)
                    act.wait_ge(var_ready, m + 1)
                    act.activation(rs[:rm, a, 1:2], rs[:rm, a, 0:1], ACT.Sqrt).then_inc(std_ready, 1)
                    if m < 2:
                        for q in (2 * m, 2 * m + 1):
                            hi_piece(act, 0, 0, q)
                    if m >= 1:
                        hi_parts(m - 1)
                    if m in (2, 4, 6, 8):
                        hi_piece(act, 1, 1, m // 2 - 1)
                    if m >= 3:
                        evac(m - 3)
                hi_parts(TILES - 1)
                for m in range(TILES - 3, TILES):
                    evac(m)

            @block.tensor
            def _(pe):
                def products(m):
                    pe.wait_ge(lo_done, 2 * (m + 1))
                    if m == 0:
                        pe.wait_ge(w_ready_hi, PIECES)
                        pe.wait_ge(w_ready_lo, PIECES)
                    if m >= 4:
                        pe.wait_ge(evac_done, m - 3)
                    tile_products(pe, 0, 0, m)

                pe.wait_ge(ident_made, 1)
                for m in range(TILES):
                    pe.wait_ge(xn_ready, m + 1)
                    if m >= 2:
                        pe.wait_ge(lo_done, 2 * (m - 1))
                    rm = rows(m)
                    for k in range(KD):
                        i = transpose(pe, bank[4 + 2 * (m % 2) + k // 4][:, (k % 4) * P:(k % 4) * P + rm],
                                      xn[:rm, m % 4, k * P:(k + 1) * P], rm)
                    i.then_inc(t_done, 1)
                    if m >= 1:
                        products(m - 1)
                products(TILES - 1)

        index = acc[:, :, :].rearrange("p t d -> p (t d)")
        used = [0]

        def carve(words, dt=F32, parts=P):
            at = used[0]
            used[0] += words
            assert used[0] <= TILES * D
            ap = index[:parts, at:at + words]
            return ap if dt == F32 else ap.bitcast(dt)

        e_src, e_dst, e_type = (carve(EC, I32, EP) for _ in range(3))
        e_loc_i, e_tile_i = carve(EC, I32, EP), carve(EC, I32, EP)
        e_srcf, e_typef, e_loc, e_tile, e_key, e_bucket = (carve(EC, F32, EP) for _ in range(6))
        e_mask, e_scan, e_pos, e_p, e_j, e_ones = (carve(EC, F32, EP) for _ in range(6))
        e_totals = carve(TILES, F32, EP)
        t_count, t_groups, t_start, t_off = (carve(TILES) for _ in range(4))
        t_int = carve(TILES, I32)
        iota_i, iota_f = carve(BLOCKS, I32), carve(BLOCKS)
        iota_h = carve(BLOCKS // 2, F16)
        tri, ones = carve(P, F32, EP), carve(P, F32, EP)
        hot_p = carve(4 * P // 2, F16, EP).rearrange("p (s n) -> p s n", s=4)
        hot_src = carve(4 * BLOCKS // 2, F16, EP).rearrange("p (s n) -> p s n", s=4)
        hot_key = carve(4 * BLOCKS // 2, F16, EP).rearrange("p (s n) -> p s n", s=4)
        hot_bucket = carve(4 * BUCKETS // 2, F16, EP).rearrange("p (s n) -> p s n", s=4)
        hot_local = carve(4 * P // 2, F16, EP).rearrange("p (s n) -> p s n", s=4)
        free_at = [0]

        def again(words, dt=F32):
            at = free_at[0]
            free_at[0] += words
            assert free_at[0] <= 17 * EC
            ap = index[:, at:at + words]
            return ap if dt == F32 else ap.bitcast(dt)

        l_key, l_keyi, l_reli = again(BLOCKS), again(BLOCKS, I32), again(BLOCKS, I32)
        l_relf, l_row, l_pad, l_tile = (again(BLOCKS) for _ in range(4))
        l_at, l_loci = again(BLOCKS), again(BLOCKS, I32)
        l_recip = again(P)

        bias_bc, gate_bc = work[:, 2048:3072], work[:, 3072:4096]
        first_ix = 2
        SRC_BANK, KEY_BANK, CNT_BANK = bank[5], bank[6], bank[7]

        with ExitStack() as stage:
            def ssem(name):
                return stage.enter_context(nc.semaphore(name))

            edges_in, bias_in, index_ready, iota_done = ssem("p_edges"), ssem("p_bias"), ssem("p_ix"), ssem("p_iota")
            tri_done, totals_done, prefix_done = ssem("p_tri"), ssem("p_totals"), ssem("p_prefix")
            hot_ready, hot_used = ssem("p_hot"), ssem("p_hotused")
            recip_made, recip_stored = ssem("p_recip"), ssem("p_recip_st")
            pool_ch, rg = ssem("p_poolch"), [ssem(f"p_rg{i}") for i in range(8)]
            block = stage.enter_context(nc.Block())

            @block.sync
            def _(sp):
                for ap, of in ((e_src, src), (e_dst, dst), (e_type, etype)):
                    sp.dma_start(ap, of).then_inc(edges_in, 16)
                sp.dma_start(bias_bc, bias[0:1, :].to_broadcast([P, D])).then_inc(bias_in, 16)
                sp.dma_start(gate_bc, b_gate[0:1, :].to_broadcast([P, D])).then_inc(bias_in, 16)

                def chunk(c, s, dest=None, prefetch=True):
                    for m in range(TILES):
                        t = TILES * s + m
                        if dest is not None:
                            sp.wait_ge(*dest[1](m))
                            sp.dma_start(dest[0](m), stage_y[:rows(m), t % 4, :]).then_inc(y_stored[t % 4], 16)
                        if m in (1, 3, 5, 7) and prefetch:
                            q = (m - 1) // 2 + 2
                            raw_free(sp, 4 * (c + 1) + q)
                            load_piece(sp, c + 1 + q // 4, q % 4)

                def y_dest(r, c, s):
                    return (lambda m: y_dram[bass.ds(r * N + m * P, rows(m)), s * HALF:(s + 1) * HALF],
                            lambda m: (evac_done, c * TILES + m + 1))

                chunk(1, 1, y_dest(0, 1, 1))
                with sp.Fori(1, R) as r:
                    for s in range(2):
                        chunk(2 * r + s, s, y_dest(r, 2 * r + s, s))
                for s in range(2):
                    chunk(CH_ROOT + s, s)
                for s in range(2):
                    chunk(CH_GATEX + s, s,
                          (lambda m, s=s: zx_dram[m * P:m * P + rows(m), s * HALF:(s + 1) * HALF],
                           lambda m, s=s: (evac_v, (2 + s) * TILES + m + 1)), prefetch=(s == 0))
                for i in range(4):
                    sp.wait_ge(y_stored[i], 16 * 5 * (R + 1))

            @block.scalar
            def _(act):
                def chunk(c, s, evac=True, split=True):
                    for m in range(TILES):
                        t = TILES * s + m
                        act.wait_ge(mm_done, c * TILES + m + 1)
                        if evac:
                            act.wait_ge(y_stored[t % 4], 16 * 5 * (c // 2 if isinstance(c, int) else r_of[0])
                                        + 16 * (t // 4))
                            act.activation(stage_y[:rows(m), t % 4, :], bank[t % 4][:rows(m), :], ACT.Copy)\
                                .then_inc(evac_done, 1)
                        if m in (1, 3, 5, 7) and split:
                            hi_piece(act, c + 1, 1 - s, (m - 1) // 2)

                r_of = [0]
                chunk(1, 1)
                with act.Fori(1, R) as r:
                    r_of[0] = r
                    for s in range(2):
                        chunk(2 * r + s, s)
                for s in range(4):
                    chunk(CH_ROOT + s, s % 2, evac=False, split=s < 3)

            @block.tensor
            def _(pe):
                def prefix():
                    pe.wait_ge(totals_done, 1)
                    pe.matmul(CNT_BANK[:, 0:TILES], tri, e_totals, start=True, stop=True)
                    pe.matmul(CNT_BANK[:, TILES:2 * TILES], ones, e_totals, start=True, stop=True)\
                        .then_inc(prefix_done, 1)

                def column(col, slot, first, last):
                    pe.wait_ge(hot_ready, col + 1)
                    pe.matmul(SRC_BANK[:, 0:BLOCKS], hot_p[:, slot, :], hot_src[:, slot, :], start=first, stop=last)
                    pe.matmul(KEY_BANK[:, 0:BLOCKS], hot_p[:, slot, :], hot_key[:, slot, :], start=first, stop=last)
                    pe.matmul(CNT_BANK[:BUCKETS, 0:P], hot_bucket[:, slot, :], hot_local[:, slot, :],
                              start=first, stop=last).then_inc(hot_used, 1)

                def chunk(c, s, cols=None, from_v=False, ends=(False, False), after_tile=None):
                    pe.wait_ge(w_ready_hi, 4 * c + 4)
                    pe.wait_ge(w_ready_lo, 4 * c + 4)
                    for m in range(TILES):
                        if from_v and (c > CH_ROOT or m >= 4):
                            pe.wait_ge(evac_v, (c - CH_ROOT) * TILES + m - 3)
                        else:
                            pe.wait_ge(evac_done, c * TILES + m - 3)
                        tile_products(pe, c, s, m)
                        if m == after_tile:
                            prefix()
                        if cols is not None:
                            for q in range(COLS_PER_TILE):
                                column(cols + m * COLS_PER_TILE + q, q, ends[0] and m == 0 and q == 0,
                                       ends[1] and m == TILES - 1 and q == COLS_PER_TILE - 1)

                chunk(1, 1, after_tile=4)
                step = TILES * COLS_PER_TILE
                for s in range(2):
                    chunk(2 + s, s, cols=s * step, ends=(s == 0, False))
                with pe.Fori(1, INDEX_CHUNKS // 2 - 1) as i:
                    for s in range(2):
                        chunk(2 * i + 2 + s, s, cols=i * (2 * step) + s * step)
                for s in range(2):
                    c = INDEX_CHUNKS + s
                    chunk(c, s, cols=(c - 2) * step, ends=(False, s == 1))
                with pe.Fori(INDEX_CHUNKS // 2 + 1, R) as i:
                    for s in range(2):
                        chunk(2 * i + s, s)
                for s in range(4):
                    chunk(CH_ROOT + s, s % 2, from_v=True)

            @block.vector
            def _(v):
                link = chained(v)

                v.wait_ge(edges_in, 48)
                v.tensor_copy(e_srcf, e_src)
                v.tensor_copy(e_typef, e_type)
                v.memset(e_ones, 1.0)
                v.tensor_scalar(e_loc_i, e_dst, P - 1, None, ALU.bitwise_and)
                link(v.tensor_scalar(e_tile_i, e_dst, P.bit_length() - 1, None, ALU.logical_shift_right))
                v.tensor_copy(e_loc, e_loc_i)
                v.tensor_copy(e_tile, e_tile_i)
                link(v.tensor_scalar(e_srcf, e_srcf, 1.0, None, ALU.add))
                v.scalar_tensor_tensor(out=e_key, in0=e_typef, scalar=float(P), in1=e_loc, op0=ALU.mult, op1=ALU.add)
                v.scalar_tensor_tensor(out=e_bucket, in0=e_tile, scalar=float(R), in1=e_typef,
                                       op0=ALU.mult, op1=ALU.add)
                link(v.memset(e_pos, -1.0))
                link(v.tensor_scalar(e_key, e_key, 1.0, None, ALU.add))
                for t in range(TILES):
                    i = v.tensor_scalar(e_mask, e_tile, float(t), 0.0, ALU.is_equal, ALU.add,
                                        accum_out=e_totals[:, t:t + 1])
                    link(i)
                v.wait_ge(iota_done, 1)
                v.tensor_copy(iota_f, iota_i)
                link(v.tensor_copy(iota_h, iota_i))
                v.memset(e_scan, 0.0).then_inc(totals_done, 1)
                for q in range(2):
                    lo_piece(v, 2, 0, q)
                v.wait_ge(prefix_done, 1)
                v.tensor_copy(t_off, CNT_BANK[:, 0:TILES])
                link(v.tensor_copy(t_count, CNT_BANK[:, TILES:2 * TILES]))
                link(v.tensor_scalar(t_count, t_count, float(GROUP * P - 1), None, ALU.add))
                link(v.tensor_copy(t_int, t_count))
                link(v.tensor_scalar(t_int, t_int, (GROUP * P).bit_length() - 1, None, ALU.logical_shift_right))
                link(v.tensor_copy(t_groups, t_int))
                link(v.memset(t_start, 0.0))
                for t in range(1, TILES):
                    link(v.tensor_tensor(t_start[:, t:t + 1], t_start[:, t - 1:t], t_groups[:, t - 1:t], ALU.add))
                link(v.scalar_tensor_tensor(out=t_off, in0=t_start, scalar=float(GROUP * P), in1=t_off,
                                            op0=ALU.mult, op1=ALU.add))
                link(v.tensor_scalar(t_start, t_start, float(GROUP), None, ALU.mult))
                for t in range(TILES):
                    link(v.tensor_scalar(e_mask, e_tile, float(t), None, ALU.is_equal))
                    link(v.tensor_tensor_scan(e_scan, e_ones, e_mask, 0.0, ALU.mult, ALU.add))
                    link(v.scalar_tensor_tensor(out=e_scan, in0=e_scan, scalar=t_off[:EP, t:t + 1], in1=e_mask,
                                                op0=ALU.add, op1=ALU.mult))
                    link(v.tensor_tensor(e_pos, e_pos, e_scan, ALU.add))
                link(v.tensor_copy(e_tile_i, e_pos))
                v.tensor_scalar(e_loc_i, e_tile_i, P - 1, None, ALU.bitwise_and)
                link(v.tensor_scalar(e_tile_i, e_tile_i, P.bit_length() - 1, None, ALU.logical_shift_right))
                v.tensor_copy(e_p, e_loc_i)
                link(v.tensor_copy(e_j, e_tile_i))

                def column(col, slot, wait):
                    if wait:
                        v.wait_ge(hot_used, col - 3)
                    at = bass.ds(col, 1)
                    v.tensor_scalar(hot_p[:, slot, :], iota_h[:EP, 0:P], e_p[:, at], None, ALU.is_equal)
                    v.tensor_scalar(hot_src[:, slot, :], iota_h[:EP, :], e_j[:, at], e_srcf[:, at],
                                    ALU.is_equal, ALU.mult)
                    v.tensor_scalar(hot_key[:, slot, :], iota_h[:EP, :], e_j[:, at], e_key[:, at],
                                    ALU.is_equal, ALU.mult)
                    v.tensor_scalar(hot_bucket[:, slot, :], iota_h[:EP, 0:BUCKETS], e_bucket[:, at], None, ALU.is_equal)
                    v.tensor_scalar(hot_local[:, slot, :], iota_h[:EP, 0:P], e_loc[:, at], None, ALU.is_equal)\
                        .then_inc(hot_ready, 1)

                def chunk(c, s, cols=None, first=False):
                    for m in range(TILES):
                        if cols is not None:
                            for q in range(COLS_PER_TILE):
                                column(cols + m * COLS_PER_TILE + q, q, not (first and m == 0))
                        if m in (1, 3, 5, 7):
                            lo_piece(v, c + 1, 1 - s, (m - 1) // 2)

                for q in range(2, PIECES):
                    lo_piece(v, 2, 0, q)
                step = TILES * COLS_PER_TILE
                for s in range(2):
                    chunk(2 + s, s, cols=s * step, first=(s == 0))
                with v.Fori(1, INDEX_CHUNKS // 2) as i:
                    for s in range(2):
                        chunk(2 * i + 2 + s, s, cols=i * (2 * step) + s * step)

                v.wait_ge(hot_used, EC)
                link(v.memset(l_recip[:, :], 0.0))
                link(v.tensor_scalar(l_recip[:BUCKETS, :], CNT_BANK[:BUCKETS, 0:P], 1.0, None, ALU.max))
                v.reciprocal(l_recip[:BUCKETS, :], l_recip[:BUCKETS, :]).then_inc(recip_made, 1)
                link(v.tensor_scalar(l_key, KEY_BANK[:, 0:BLOCKS], -1.0, None, ALU.add))
                link(v.tensor_copy(l_keyi, l_key))
                v.tensor_scalar(l_reli, l_keyi, P.bit_length() - 1, None, ALU.arith_shift_right)
                link(v.tensor_scalar(l_loci, l_keyi, P - 1, None, ALU.bitwise_and))
                v.tensor_copy(sort_local[:, :], l_loci)
                link(v.tensor_copy(l_relf, l_reli))
                link(v.scalar_tensor_tensor(out=l_row, in0=l_relf, scalar=float(N), in1=SRC_BANK[:, 0:BLOCKS],
                                            op0=ALU.mult, op1=ALU.add))
                link(v.tensor_scalar(l_pad, l_key, 0.0, float(Y_PAD), ALU.is_lt, ALU.mult))
                link(v.scalar_tensor_tensor(out=l_row, in0=l_row, scalar=-1.0, in1=l_pad, op0=ALU.add, op1=ALU.add))
                v.tensor_copy(sort_row[:, :], l_row)
                link(v.memset(l_tile, 0.0))
                for t in range(1, TILES):
                    link(v.scalar_tensor_tensor(out=l_tile, in0=iota_f, scalar=t_start[:, t:t + 1], in1=l_tile,
                                                op0=ALU.is_ge, op1=ALU.add))
                v.tensor_copy(group_tile[:, :], l_tile.rearrange("p (g b) -> p g b", b=GROUP)[:, :, 0])
                link(v.scalar_tensor_tensor(out=l_at, in0=l_tile, scalar=float(R * P), in1=l_key,
                                            op0=ALU.mult, op1=ALU.add))
                link(v.tensor_scalar(l_pad, l_key, 0.0, None, ALU.is_ge))
                link(v.scalar_tensor_tensor(out=l_at, in0=l_at, scalar=-float(BUCKETS * P), in1=l_pad,
                                            op0=ALU.add, op1=ALU.mult))
                link(v.tensor_scalar(l_at, l_at, float(BUCKETS * P), None, ALU.add))
                v.tensor_copy(recip_at[:, :], l_at).then_inc(index_ready, 1)

                with v.Fori(INDEX_CHUNKS // 2 + 1, R) as i:
                    for s in range(2):
                        chunk(2 * i + s, s)
                v.wait_ge(bias_in, 32)
                v.wait_ge(recip_stored, 16)
                link(v.memset(acc[:, TILES - 1, :], 0.0))
                for s in range(4):
                    c = CH_ROOT + s
                    for m in range(TILES):
                        t, h = TILES * (s % 2) + m, s % 2
                        v.wait_ge(mm_done, c * TILES + m + 1)
                        if s < 2:
                            v.tensor_tensor(acc[:rows(m), m, h * HALF:(h + 1) * HALF], bank[t % 4][:rows(m), :],
                                            bias_bc[:rows(m), h * HALF:(h + 1) * HALF], ALU.add).then_inc(evac_v, 1)
                        else:
                            v.wait_ge(y_stored[t % 4], 16 * 5 * R + 16 * (t // 4))
                            v.tensor_tensor(stage_y[:rows(m), t % 4, :], bank[t % 4][:rows(m), :],
                                            gate_bc[:rows(m), h * HALF:(h + 1) * HALF], ALU.add).then_inc(evac_v, 1)
                        if m in (1, 3, 5, 7) and s < 3:
                            lo_piece(v, c + 1, 1 - s % 2, (m - 1) // 2)

            @block.gpsimd
            def _(pool):
                pool.memset(tri, 1.0).then_inc(pool_ch, 1)
                pool.memset(ones, 1.0).then_inc(pool_ch, 1)
                pool.memset(gate_word[:, :], 0.0).then_inc(pool_ch, 1)
                pool.wait_ge(pool_ch, 3)
                pool.affine_select(out=tri, in_=tri, compare_op=ALU.is_gt, fill=0.0, base=0,
                                   pattern=[[1, P]], channel_multiplier=-1).then_inc(pool_ch, 1)
                pool.iota(iota_i, pattern=[[1, BLOCKS]], base=0, channel_multiplier=0).then_inc(iota_done, 1)
                pool.wait_ge(recip_made, 1)
                pool.dma_start(recip_dram.rearrange("(b p) o -> b (p o)", p=P), l_recip[:BUCKETS + 1, :])\
                    .then_inc(recip_stored, 16)
                pool.wait_ge(recip_stored, 16)
                pool.wait_ge(index_ready, 1)
                pool.wait_ge(pool_ch, 4)
                with pool.Fori(0, BLOCKS // 8) as i:
                    pool.tensor_copy(l_slot_i[:, :], recip_at[:, bass.ds(i * 8, 8)]).then_inc(pool_ch, 1)
                    pool.wait_ge(pool_ch, 2 * i + 5)
                    pool.tensor_tensor(gate_word[:, 1:2], gate_word[:, 0:1], gate_word[:, 0:1], ALU.add)
                    for q in range(8):
                        pool.indirect_dma_start(l_slot_r[:, q:q + 1], None, recip_dram,
                                                IndirectOffsetOnAxis(ap=l_slot_i[:, q:q + 1], axis=0))\
                            .then_inc(rg[q], 16)
                    for q in range(8):
                        pool.wait_ge(rg[q], 16 * i + 16)
                    pool.tensor_copy(sort_recip[:, bass.ds(i * 8, 8)], l_slot_r[:, :]).then_inc(pool_ch, 1)
                    pool.wait_ge(pool_ch, 2 * i + 6)

        operands.close()

        SLOTS = 16
        PASSES = BLOCKS // SLOTS
        PASS_GROUPS = SLOTS // GROUP
        SPLITS = 2
        DIRECTS = GROUP - SPLITS
        assert BLOCKS % SLOTS == 0 and PASS_GROUPS % 2 == 0
        with ExitStack() as stage:
            def ssem(name):
                return stage.enter_context(nc.semaphore(name))

            def ssb(name, shape, dt=F32):
                return stage.enter_context(nc.sbuf_tensor(name, shape, dt))

            y_in = ssb("y_in", [P, SLOTS, D])
            y_hi, y_lo = ssb("y_hi", [P, SPLITS, D], F32R), ssb("y_lo", [P, SPLITS, D], F32R)
            hot = ssb("hot", [P, SPLITS, P], F32R)
            hot_scaled = ssb("hot_scaled", [P, 2 * DIRECTS, P])
            lanes = ssb("lanes", [P, P])
            lanes_i = ssb("lanes_i", [P, P], I32)
            row_s, recip_s, local_s = ssb("row_s", [P, SLOTS], I32), ssb("recip_s", [P, SLOTS]), ssb("local_s", [P, SLOTS])

            got = [ssem(f"g_got{b}") for b in range(SLOTS)]
            hi_done, v_done, pe_done = ssem("g_hi"), ssem("g_v"), ssem("g_pe")
            cleared_p = ssem("g_clearp")
            VECTOR_CLEARS = [b for b in range(SLOTS) if b // GROUP % 2 == 0]
            cleared, lanes_done, copied = ssem("g_clear"), ssem("g_lanes"), ssem("g_copied")
            flushed = [ssem("g_flush0"), ssem("g_flush1")]
            block = stage.enter_context(nc.Block())

            @block.sync
            def _(sp):
                for n in range(2, 2 * PIECES):
                    c, q = CH_GATEU + n // PIECES, n % PIECES
                    raw_free(sp, PIECES * c + q)
                    load_piece(sp, c, q)

            @block.gpsimd
            def _(pool):
                pool.iota(lanes_i[:, :], pattern=[[1, P]], base=0, channel_multiplier=0).then_inc(lanes_done, 1)

                def clear(h):
                    for b in range(h * GROUP, (h + 1) * GROUP):
                        pool.memset(y_in[:, b, :], 0.0).then_inc(cleared_p, 1)

                clear(1)

                def one_pass(i):
                    for h in range(PASS_GROUPS):
                        if isinstance(i, int) and h == 3:
                            clear(3)
                        part = slice(h * GROUP, (h + 1) * GROUP)
                        for b in range(h * GROUP, (h + 1) * GROUP):
                            wait_after_first(pool, got[b], 16 * i)
                        if not isinstance(i, int):
                            pool.wait_ge(v_done, SLOTS * i + (h + 1) * GROUP - SLOTS)
                            pool.wait_ge(pe_done, SLOTS * i + (h + 1) * GROUP - SLOTS)
                        at = bass.ds(i * SLOTS + h * GROUP, GROUP)
                        pool.tensor_copy(recip_s[:, part], sort_recip[:, at]).then_inc(copied, 1)
                        pool.tensor_copy(local_s[:, part], sort_local[:, at]).then_inc(copied, 1)
                        pool.tensor_copy(row_s[:, part], sort_row[:, at]).then_inc(copied, 1)
                        pool.wait_ge(copied, 3 * PASS_GROUPS * i + 3 * h + 3)
                        if isinstance(i, int):
                            pool.wait_ge(cleared, GROUP * (1 + h // 2))
                            pool.wait_ge(cleared_p, GROUP * ((h + 1) // 2))
                        pool.tensor_tensor(gate_word[:, 1:2], gate_word[:, 0:1], gate_word[:, 0:1], ALU.add)
                        for b in range(h * GROUP, (h + 1) * GROUP):
                            pool.indirect_dma_start(y_in[:, b, :], None, y_dram,
                                                    IndirectOffsetOnAxis(ap=row_s[:, b:b + 1], axis=0),
                                                    bounds_check=R * N - 1, oob_is_err=False)\
                                .then_inc(got[b], 16)

                one_pass(0)
                with pool.Fori(1, PASSES) as i:
                    one_pass(i)

            def slot_wait(eng, i, b):
                if not isinstance(i, int) or b >= GROUP:
                    eng.wait_ge(pe_done, SLOTS * i + b - GROUP + 1)

            @block.scalar
            def _(act):
                def one_pass(i, pieces=False):
                    for b in range(SLOTS):
                        s = b % GROUP
                        if pieces and b % 2 == 1:
                            hi_piece(act, CH_GATEU + b // 8, b // 8, (b // 2) % PIECES)
                        if s >= SPLITS:
                            continue
                        act.wait_ge(got[b], 16 * i + 16)
                        act.wait_ge(copied, 3 * PASS_GROUPS * i + 3 * (b // GROUP) + 3)
                        slot_wait(act, i, b)
                        act.activation(y_hi[:, s, :], y_in[:, b, :], ACT.Copy, scale=recip_s[:, b:b + 1])\
                            .then_inc(hi_done, 1)

                one_pass(0, pieces=True)
                with act.Fori(1, PASSES) as i:
                    one_pass(i)

            @block.vector
            def _(v):
                link = chained(v)
                for b in VECTOR_CLEARS:
                    v.memset(y_in[:, b, :], 0.0).then_inc(cleared, 1)
                v.wait_ge(lanes_done, 1)
                link(v.tensor_copy(lanes[:, :], lanes_i[:, :]))

                def blocks(i, h, pieces):
                    for b in range(h * GROUP, (h + 1) * GROUP):
                        s = b % GROUP
                        if pieces and b % 2 == 1:
                            lo_piece(v, CH_GATEU + b // 8, b // 8, (b // 2) % PIECES)
                        v.wait_ge(copied, 3 * PASS_GROUPS * i + 3 * h + 3)
                        if s >= SPLITS:
                            if not isinstance(i, int) or b >= 2 * GROUP:
                                v.wait_ge(pe_done, SLOTS * i + b - 2 * GROUP + 1)
                            v.tensor_scalar(hot_scaled[:, h % 2 * DIRECTS + s - SPLITS, :], lanes[:, :], local_s[:, b:b + 1],
                                            recip_s[:, b:b + 1], ALU.is_equal, ALU.mult).then_inc(v_done, 1)
                        else:
                            slot_wait(v, i, b)
                            v.tensor_scalar(hot[:, s, :], lanes[:, :], local_s[:, b:b + 1], None, ALU.is_equal)
                            v.wait_ge(hi_done, SPLITS * PASS_GROUPS * i + SPLITS * h + s + 1)
                            v.scalar_tensor_tensor(out=y_lo[:, s, :], in0=y_in[:, b, :], scalar=recip_s[:, b:b + 1],
                                                   in1=y_hi[:, s, :].bitcast(F32), op0=ALU.mult, op1=ALU.subtract)\
                                .then_inc(v_done, 1)

                def flush(g, h, at_pass):
                    v.wait_ge(pe_done, GROUP * g + GROUP)
                    tile = v.value_load(group_tile[0:1, bass.ds(g, 1)], min_val=0, max_val=TILES - 1)
                    for q in range(2):
                        u = acc[:, bass.ds(tile, 1), q * HALF:(q + 1) * HALF].rearrange("p o n -> p (o n)")
                        last = v.tensor_tensor(u, u, bank[2 * h + q][:, :], ALU.add)
                    last.then_inc(flushed[h], 1)
                    v.wait_ge(flushed[h], at_pass)

                def one_pass(i, pieces=False):
                    for h in range(PASS_GROUPS):
                        blocks(i, h, pieces)
                        if h > 0 or not isinstance(i, int):
                            g = PASS_GROUPS * i + h - 1
                            k = (h - 1) // 2 if h else -1
                            flush(g, (h - 1) % 2, PASS_GROUPS // 2 * i + k + 1)

                one_pass(0, pieces=True)
                with v.Fori(1, PASSES) as i:
                    one_pass(i)
                flush(GROUPS - 1, 1, GROUPS // 2)

            @block.tensor
            def _(pe):
                def one_pass(i):
                    for g in range(PASS_GROUPS):
                        h = g % 2
                        wait_after_first(pe, flushed[h], PASS_GROUPS // 2 * i + g // 2)
                        for b in range(g * GROUP, (g + 1) * GROUP):
                            s = b % GROUP
                            pe.wait_ge(v_done, SLOTS * i + b + 1)
                            if s >= SPLITS:
                                pe.wait_ge(got[b], 16 * i + 16)
                                for q in range(2):
                                    m = pe.matmul(bank[2 * h + q][:, :], hot_scaled[:, h * DIRECTS + s - SPLITS, :],
                                                  y_in[:, b, q * HALF:(q + 1) * HALF],
                                                  start=False, stop=(s == GROUP - 1))
                            else:
                                for y in (y_hi, y_lo):
                                    for q in range(2):
                                        m = pe.matmul(bank[2 * h + q][:, :], hot[:, s, :],
                                                      y[:, s, q * HALF:(q + 1) * HALF],
                                                      start=(s == 0 and y is y_hi), stop=False)
                            m.then_inc(pe_done, 1)

                one_pass(0)
                with pe.Fori(1, PASSES) as i:
                    one_pass(i)
        sorting.close()

        opT = ctx.enter_context(ExitStack())
        opT_hi = opT.enter_context(nc.sbuf_tensor("opT_hi", [P, KD, N], F32R))
        opT_lo = opT.enter_context(nc.sbuf_tensor("opT_lo", [P, KD, N], F32R))
        with ExitStack() as stage:
            def ssem(name):
                return stage.enter_context(nc.semaphore(name))

            def ssb(name, shape, dt=F32):
                return stage.enter_context(nc.sbuf_tensor(name, shape, dt))

            x_s = ssb("x_s", [P, 2, D])
            z_s = ssb("z_s", [P, 2, D])
            th = w_raw
            lgT = ssb("lgT", [E, N])

            x_in, zx_in = [ssem("z_x0"), ssem("z_x1")], [ssem("z_zx0"), ssem("z_zx1")]
            wr_in, wr_done = ssem("z_wr"), ssem("z_wrdone")
            uT_done, uhi, ulo = ssem("z_uT"), ssem("z_uhi"), ssem("z_ulo")
            tT_done, thi, tlo = ssem("z_tT"), ssem("z_thi"), ssem("z_tlo")
            tanh_done, z_done, z_read = ssem("z_tanh"), ssem("z_z"), ssem("z_zread")
            var_ready, std_ready = ssem("z_var"), ssem("z_std")
            x1_ready, t_ready, lg_done, lg_out = ssem("z_x1r"), ssem("z_t"), ssem("z_lg"), ssem("z_lgout")
            x1_stored = [ssem("z_st0"), ssem("z_st1")]
            t_stored, lg_rows = ssem("z_tst"), ssem("z_lgrows")
            block = stage.enter_context(nc.Block())

            def load_rows(sp, m):
                at = slice(m * P, m * P + rows(m))
                sp.dma_start(x_s[:rows(m), m % 2, :], x[at, :]).then_inc(x_in[m % 2], 16)
                sp.dma_start(z_s[:rows(m), m % 2, :], zx_dram[at, :]).then_inc(zx_in[m % 2], 16)

            def store_rows(sp, m):
                sp.wait_ge(t_ready, m + 1)
                at = slice(m * P, m * P + rows(m))
                sp.dma_start(x1_dram[at, :], x_s[:rows(m), m % 2, :]).then_inc(x1_stored[m % 2], 16)
                sp.dma_start(t_dram[at, :], acc[:rows(m), m, :]).then_inc(t_stored, 16)

            @block.sync
            def _(sp):
                load_rows(sp, 0)
                sp.dma_start(wr_raw[:, :, :], wr).then_inc(wr_in, 16)
                sp.dma_start(br_bc[:, :], br[0:1, :].to_broadcast([P, E])).then_inc(wr_in, 16)
                sp.dma_start(b1_sb[:, :, :], b1).then_inc(wr_in, 16)
                load_rows(sp, 1)
                for m in range(2, TILES):
                    store_rows(sp, m - 2)
                    sp.wait_ge(x1_stored[m % 2], 16 * (m // 2))
                    load_rows(sp, m)
                store_rows(sp, TILES - 2)
                store_rows(sp, TILES - 1)
                for i in range(2):
                    sp.wait_ge(x1_stored[i], 16 * (TILES // 2))
                sp.wait_ge(t_stored, 16 * TILES)

            @block.scalar
            def _(act):
                act.wait_ge(wr_in, 48)
                act.activation(wr_hi[:, :, :], wr_raw[:, :, :], ACT.Copy).then_inc(wr_done, 1)

                def hi(m, done, out_sem, b):
                    act.wait_ge(done, m + 1)
                    for q in range(2):
                        act.activation(opT_hi[:, 4 * q:4 * q + 4, m * P:m * P + rows(m)], four(b + q, rows(m)), ACT.Copy)\
                            .then_inc(out_sem, 1)

                for s in range(-1, TILES + 2):
                    if s + 1 < TILES:
                        hi(s + 1, uT_done, uhi, 4)
                    if 0 <= s < TILES:
                        if s >= 2:
                            act.wait_ge(x1_ready, s - 1)
                        act.activation(th[:rows(s), s % 2, :], acc[:rows(s), s, :], ACT.Tanh).then_inc(tanh_done, 1)
                    if 0 <= s - 1 < TILES:
                        hi(s - 1, tT_done, thi, 6)
                    if 0 <= s - 2 < TILES:
                        act.wait_ge(lg_done, s - 1)
                        act.activation(lgT[:, (s - 2) * P:(s - 2) * P + rows(s - 2)], bank[4][:E, 0:rows(s - 2)],
                                       ACT.Copy).then_inc(lg_out, 1)
                    if 0 <= s < TILES:
                        act.wait_ge(var_ready, s + 1)
                        act.activation(rs[:rows(s), s % 2, 1:2], rs[:rows(s), s % 2, 0:1], ACT.Sqrt)\
                            .then_inc(std_ready, 1)
                act.wait_ge(lg_rows, 1)
                act.activation(router[:, 0:TILES - 1, :].rearrange("p m e -> p (m e)"),
                               bank[0][:, 0:(TILES - 1) * E], ACT.Copy)
                act.activation(router[:rows(TILES - 1), TILES - 1, :],
                               bank[0][:rows(TILES - 1), (TILES - 1) * E:TILES * E], ACT.Copy)

            @block.tensor
            def _(pe):
                def transposed(m, b, done):
                    for k in range(KD):
                        t = transpose(pe, bank[b + k // 4][:, (k % 4) * P:(k % 4) * P + rows(m)],
                                      acc[:rows(m), m, k * P:(k + 1) * P], rows(m))
                    t.then_inc(done, 1)

                for s in range(-1, TILES + 2):
                    if s + 1 < TILES:
                        if s >= 0:
                            pe.wait_ge(ulo, 2 * (s + 1))
                        if s - 3 >= 0:
                            pe.wait_ge(lg_out, s - 2)
                        transposed(s + 1, 4, uT_done)
                    if 0 <= s < TILES:
                        pe.wait_ge(uhi, 2 * s + 2)
                        pe.wait_ge(ulo, 2 * s + 2)
                        if s >= 2:
                            pe.wait_ge(z_read, s - 1)
                        rm, b = rows(s), 2 * (s % 2)
                        for q in range(2):
                            n = 0
                            for a_, b_ in ((opT_hi, w_hi), (opT_hi, w_lo), (opT_lo, w_hi)):
                                for k in range(KD):
                                    i = pe.matmul(bank[b + q][:rm, :], a_[:, k, s * P:s * P + rm],
                                                  b_[:, q, k * HALF:(k + 1) * HALF],
                                                  start=(n == 0), stop=(n == 3 * KD - 1))
                                    n += 1
                        i.then_inc(z_done, 1)
                    if 0 <= s - 1 < TILES:
                        pe.wait_ge(t_ready, s)
                        if s - 2 >= 0:
                            pe.wait_ge(tlo, 2 * (s - 1))
                        transposed(s - 1, 6, tT_done)
                    if 0 <= s - 2 < TILES:
                        m = s - 2
                        pe.wait_ge(ulo, 2 * min(s + 2, TILES))
                        pe.wait_ge(thi, 2 * m + 2)
                        pe.wait_ge(tlo, 2 * m + 2)
                        pe.wait_ge(wr_done, 2)
                        if m >= 1:
                            pe.wait_ge(lg_out, m)
                        n = 0
                        for w_, x_ in ((wr_hi, opT_hi), (wr_lo, opT_hi), (wr_hi, opT_lo)):
                            for k in range(KD):
                                i = pe.matmul(bank[4][:E, 0:rows(m)], w_[:, k, :], x_[:, k, m * P:m * P + rows(m)],
                                              start=(n == 0), stop=(n == 3 * KD - 1))
                                n += 1
                        i.then_inc(lg_done, 1)
                pe.wait_ge(lg_out, TILES)
                pe.wait_ge(z_read, TILES)
                for m in range(TILES):
                    i = transpose(pe, bank[0][:rows(m), m * E:(m + 1) * E], lgT[:, m * P:m * P + rows(m)], E)
                i.then_inc(lg_rows, 1)

            @block.vector
            def _(v):
                link = chained(v)

                link(v.memset(router[:, :, :], 0.0))
                v.wait_ge(wr_done, 1)
                v.tensor_tensor(wr_lo[:, :, :], wr_raw[:, :, :], wr_hi[:, :, :].bitcast(F32), ALU.subtract)\
                    .then_inc(wr_done, 1)

                def lo(m, hi_sem, out_sem, b):
                    for q in range(2):
                        v.wait_ge(hi_sem, 2 * m + q + 1)
                        cols = slice(m * P, m * P + rows(m))
                        v.tensor_tensor(opT_lo[:, 4 * q:4 * q + 4, cols], four(b + q, rows(m)),
                                        opT_hi[:, 4 * q:4 * q + 4, cols].bitcast(F32), ALU.subtract)\
                            .then_inc(out_sem, 1)

                for s in range(-1, TILES + 1):
                    if s + 1 < TILES:
                        lo(s + 1, uhi, ulo, 4)
                    if 0 <= s < TILES:
                        rm, a = rows(s), s % 2
                        xs, zs, ts, u = x_s[:rm, a, :], z_s[:rm, a, :], th[:rm, a, :], acc[:rm, s, :]
                        v.wait_ge(x_in[a], 16 * (s // 2 + 1))
                        v.wait_ge(tanh_done, s + 1)
                        v.wait_ge(uT_done, s + 1)
                        link(v.tensor_scalar(u, xs, mean_all[:rm, s:s + 1], rstd_all[:rm, s:s + 1],
                                             ALU.subtract, ALU.mult))
                        v.tensor_tensor(ts, ts, u, ALU.subtract)
                        link(v.tensor_tensor(xs, xs, u, ALU.add))
                        v.wait_ge(zx_in[a], 16 * (s // 2 + 1))
                        v.wait_ge(z_done, s + 1)
                        for q in range(2):
                            i = v.tensor_tensor(zs[:, q * HALF:(q + 1) * HALF], zs[:, q * HALF:(q + 1) * HALF],
                                                bank[2 * a + q][:rm, :], ALU.add)
                        i.then_inc(z_read, 1)
                        v.wait_ge(z_read, s + 1)
                        link(v.tensor_tensor(ts, ts, zs, ALU.mult))
                        v.tensor_tensor(xs, xs, ts, ALU.add).then_inc(x1_ready, 1)
                        v.wait_ge(x1_ready, s + 1)
                        norm_stats(v, link, xs, a, rm, var_ready)
                        v.wait_ge(std_ready, s + 1)
                        rstd(v, link, a, rm, rs[:rm, a, 3:4])
                        v.tensor_scalar(u, xs, aggr[:rm, a, 0:1], rs[:rm, a, 3:4], ALU.subtract, ALU.mult)\
                            .then_inc(t_ready, 1)
                    if 0 <= s - 1 < TILES:
                        lo(s - 1, thi, tlo, 6)

        opT.close()

        COLS = 2 * TILES
        routing = ctx.enter_context(ExitStack())

        def route_sb(name, shape, dt=F32):
            return routing.enter_context(nc.sbuf_tensor(name, shape, dt))

        weight_of = route_sb("weight_of", [P, 2, TILES])
        place_i = route_sb("place_i", [P, COLS], I32)
        token_at = route_sb("token_at", [P, TILES_T], I32)
        expert_of = route_sb("expert_of", [P, BLOCKS_T], I32)
        RAW = 2 * PIECES
        e_raw = route_sb("e_rawbuf", [P, RAW, PIECE])
        t_s = route_sb("t_s", [P, 2, D])
        raw_in = [sem(f"e_raw{i}") for i in range(RAW)]
        expert_ready = sem("r_expert")

        def expert(eng, b):
            return eng.value_load(expert_of[0:1, bass.ds(b, 1)], min_val=0, max_val=E - 1)

        def load_expert(sp, e, q):
            sp.dma_start(e_raw[:, q, :], wchunks[bass.ds(e * (2 * P) + (CH_EXP + q // PIECES) * P, P),
                                                 (q % PIECES) * PIECE:(q % PIECES + 1) * PIECE]).then_inc(raw_in[q], 16)

        with ExitStack() as stage:
            def ssem(name):
                return stage.enter_context(nc.semaphore(name))

            def ssb(name, shape, dt=F32):
                return stage.enter_context(nc.sbuf_tensor(name, shape, dt))

            r_tri, r_ones = ssb("r_tri", [P, P]), ssb("r_ones", [P, P])
            lane_i, lane_f = ssb("lane_i", [P, P], I32), ssb("lane_f", [P, P])
            before_i, before = ssb("before_i", [P, E, E], I32), ssb("before", [P, E, E])
            token_i, token_f = ssb("token_i", [P, TILES], I32), ssb("token_f", [P, TILES])
            over, same = ssb("over", [P, TILES, E, E]), ssb("same", [P, TILES, E, E])
            rank, chosen = ssb("rank", [P, TILES, E]), ssb("chosen", [P, COLS, E])
            top, low, ex, valid = ssb("top", [P, TILES]), ssb("low", [P, TILES]), ssb("ex", [P, TILES]), ssb("valid", [P, 1])
            prefix, total = ssb("prefix", [P, COLS, E]), ssb("total", [P, COLS, E])
            running = ssb("running", [P, E, COLS])
            ones_c = ssb("ones_c", [P, COLS])
            blocks_f, blocks_i = ssb("blocks_f", [P, E]), ssb("blocks_i", [P, E], I32)
            block_end, start = ssb("block_end", [P, E]), ssb("start", [P, E])
            place = ssb("place", [P, COLS])
            low_i, high_i = ssb("low_i", [P, COLS], I32), ssb("high_i", [P, COLS], I32)
            low_f, high_f = ssb("low_f", [P, COLS]), ssb("high_f", [P, COLS])
            hot_low = ssb("hot_low", [P, COLS, P], F16)
            hot_high, hot_token = ssb("hot_high", [P, COLS, TILES_T]), ssb("hot_token", [P, COLS, TILES_T], F16)
            listed, empty = ssb("listed", [P, TILES_T]), ssb("empty", [P, TILES_T])
            past = ssb("past", [P, BLOCKS_T, E - 1])
            made, exp_in, exp_out = ssem("r_made"), ssem("r_expin"), ssem("r_expout")
            chosen_ready, counted, hot_ready, list_done = ssem("r_chosen"), ssem("r_counted"), ssem("r_hot"), ssem("r_list")
            block = stage.enter_context(nc.Block())

            @block.gpsimd
            def _(pool):
                pool.memset(r_tri[:, :], 1.0).then_inc(made, 1)
                pool.memset(r_ones[:, :], 1.0).then_inc(made, 1)
                pool.iota(lane_i[:, :], pattern=[[1, P]], base=0, channel_multiplier=0).then_inc(made, 1)
                pool.iota(before_i[:, :, :], pattern=[[-1, E], [1, E]], base=0, channel_multiplier=0).then_inc(made, 1)
                pool.iota(token_i[:, :], pattern=[[P, TILES]], base=1, channel_multiplier=1).then_inc(made, 1)
                pool.wait_ge(made, 5)
                pool.affine_select(out=r_tri[:, :], in_=r_tri[:, :], compare_op=ALU.is_gt, fill=0.0, base=0,
                                   pattern=[[1, P]], channel_multiplier=-1).then_inc(made, 1)
                pool.memset(t_s[:, :, :], 0.0).then_inc(made, 1)

            @block.sync
            def _(sp):
                sp.wait_ge(expert_ready, 1)
                e = expert(sp, 0)
                for q in range(RAW):
                    load_expert(sp, e, q)

            @block.scalar
            def _(act):
                act.wait_ge(exp_in, 1)
                act.activation(ex[:, :], low[:, :], ACT.Exp).then_inc(exp_out, 1)

            @block.tensor
            def _(pe):
                flat = chosen[:, :, :].rearrange("p c e -> p (c e)")
                pe.wait_ge(made, 6)
                pe.wait_ge(chosen_ready, 2)
                pe.matmul(bank[0][:, 0:COLS * E], r_tri[:, :], flat, start=True, stop=True)
                pe.matmul(bank[1][:, 0:COLS * E], r_ones[:, :], flat, start=True, stop=True).then_inc(counted, 1)
                pe.wait_ge(hot_ready, 1)
                for c in range(COLS):
                    rm = rows(c % TILES)
                    i = pe.matmul(bank[2][:, 0:TILES_T], hot_low[:rm, c, :], hot_token[:rm, c, :],
                                  start=(c == 0), stop=(c == COLS - 1))
                i.then_inc(list_done, 1)

            @block.vector
            def _(v):
                link = chained(v)

                four_d = [P, TILES, E, E]
                lg = router[:, :, :]
                link(v.tensor_tensor(lg, lg, br_bc[:, :].unsqueeze(1).to_broadcast([P, TILES, E]), ALU.add))
                v.reduce_max(top[:, :], lg, axis=AX.X)
                mine, other = lg.unsqueeze(3).to_broadcast(four_d), lg.unsqueeze(2).to_broadcast(four_d)
                v.tensor_tensor(over[:, :, :, :], other, mine, ALU.is_gt)
                v.tensor_tensor(same[:, :, :, :], other, mine, ALU.is_equal)
                v.wait_ge(made, 6)
                v.tensor_copy(before[:, :, :], before_i[:, :, :])
                v.tensor_copy(token_f[:, :], token_i[:, :])
                v.memset(ones_c[:, :], 1.0)
                link(v.tensor_copy(lane_f[:, :], lane_i[:, :]))
                link(v.tensor_scalar(before[:, :, :], before[:, :, :], 0.0, None, ALU.is_lt))
                link(v.tensor_tensor(same[:, :, :, :], same[:, :, :, :],
                                     before[:, :, :].unsqueeze(1).to_broadcast(four_d), ALU.mult))
                link(v.tensor_tensor(over[:, :, :, :], over[:, :, :, :], same[:, :, :, :], ALU.add))
                v.tensor_scalar(valid[:, :], token_f[:, TILES - 1:TILES], float(N), None, ALU.is_le)
                link(v.reduce_sum(rank[:, :, :], over[:, :, :, :], axis=AX.X))
                for k in range(2):
                    i = v.tensor_scalar(chosen[:, k * TILES:(k + 1) * TILES, :], rank[:, :, :], float(k), None, ALU.is_equal)
                link(i)
                link(v.tensor_tensor(rank[:, :, :], chosen[:, TILES:COLS, :], lg, ALU.mult))
                link(v.reduce_sum(low[:, :], rank[:, :, :], axis=AX.X))
                v.tensor_tensor(low[:, :], low[:, :], top[:, :], ALU.subtract).then_inc(exp_in, 1)
                for k in range(2):
                    at = chosen[:, (k + 1) * TILES - 1, :]
                    v.tensor_scalar(at, at, valid[:, 0:1], None, ALU.mult).then_inc(chosen_ready, 1)
                v.wait_ge(exp_out, 1)
                link(v.tensor_scalar(top[:, :], ex[:, :], 1.0, None, ALU.add))
                link(v.reciprocal(weight_of[:, 0, :], top[:, :]))
                v.tensor_tensor(weight_of[:, 1, :], ex[:, :], weight_of[:, 0, :], ALU.mult)
                v.wait_ge(counted, 1)
                v.tensor_copy(prefix[:, :, :].rearrange("p c e -> p (c e)"), bank[0][:, 0:COLS * E])
                link(v.tensor_copy(total[:, :, :].rearrange("p c e -> p (c e)"), bank[1][:, 0:COLS * E]))
                for e in range(E):
                    i = v.tensor_tensor_scan(running[:, e, :], ones_c[:, :], total[:, :, e], 0.0, ALU.mult, ALU.add)
                link(i)
                link(v.tensor_scalar(blocks_f[:, :], running[:, :, COLS - 1], float(BLOCK_T - 1), None, ALU.add))
                link(v.tensor_copy(blocks_i[:, :], blocks_f[:, :]))
                link(v.tensor_scalar(blocks_i[:, :], blocks_i[:, :], BLOCK_T.bit_length() - 1, None, ALU.logical_shift_right))
                link(v.tensor_copy(blocks_f[:, :], blocks_i[:, :]))
                link(v.tensor_tensor_scan(block_end[:, :], ones_c[:, 0:E], blocks_f[:, :], 0.0, ALU.mult, ALU.add))
                v.tensor_tensor(prefix[:, :, :], prefix[:, :, :], total[:, :, :], ALU.subtract)
                link(v.tensor_tensor(start[:, :], block_end[:, :], blocks_f[:, :], ALU.subtract))
                link(v.tensor_tensor(past[:, :, :], lane_f[:, 0:BLOCKS_T].unsqueeze(2).to_broadcast([P, BLOCKS_T, E - 1]),
                                     start[:, 1:E].unsqueeze(1).to_broadcast([P, BLOCKS_T, E - 1]), ALU.is_ge))
                link(v.reduce_sum(listed[:, 0:BLOCKS_T], past[:, :, :], axis=AX.X))
                v.tensor_copy(expert_of[:, :], listed[:, 0:BLOCKS_T]).then_inc(expert_ready, 1)
                link(v.tensor_tensor(prefix[:, :, :], prefix[:, :, :], running[:, :, :].rearrange("p e c -> p c e"), ALU.add))
                link(v.scalar_tensor_tensor(out=prefix[:, :, :], in0=start[:, :].unsqueeze(1).to_broadcast([P, COLS, E]),
                                            scalar=float(BLOCK_T), in1=prefix[:, :, :], op0=ALU.mult, op1=ALU.add))
                link(v.tensor_tensor(prefix[:, :, :], prefix[:, :, :], chosen[:, :, :], ALU.mult))
                link(v.reduce_sum(place[:, :], prefix[:, :, :], axis=AX.X))
                link(v.tensor_copy(place_i[:, :], place[:, :]))
                v.tensor_scalar(low_i[:, :], place_i[:, :], P - 1, None, ALU.bitwise_and)
                link(v.tensor_scalar(high_i[:, :], place_i[:, :], P.bit_length() - 1, None, ALU.logical_shift_right))
                v.tensor_copy(low_f[:, :], low_i[:, :])
                link(v.tensor_copy(high_f[:, :], high_i[:, :]))
                v.tensor_tensor(hot_low[:, :, :], lane_f[:, :].unsqueeze(1).to_broadcast([P, COLS, P]),
                                low_f[:, :].unsqueeze(2).to_broadcast([P, COLS, P]), ALU.is_equal)
                link(v.tensor_tensor(hot_high[:, :, :], lane_f[:, 0:TILES_T].unsqueeze(1).to_broadcast([P, COLS, TILES_T]),
                                     high_f[:, :].unsqueeze(2).to_broadcast([P, COLS, TILES_T]), ALU.is_equal))
                for k in range(2):
                    at = slice(k * TILES, (k + 1) * TILES)
                    i = v.tensor_tensor(hot_token[:, at, :], hot_high[:, at, :],
                                        token_f[:, :].unsqueeze(2).to_broadcast([P, TILES, TILES_T]), ALU.mult)
                i.then_inc(hot_ready, 1)
                v.wait_ge(list_done, 1)
                link(v.tensor_scalar(empty[:, :], bank[2][:, 0:TILES_T], 0.0, float(Y_PAD), ALU.is_equal, ALU.mult))
                link(v.scalar_tensor_tensor(out=listed[:, :], in0=bank[2][:, 0:TILES_T], scalar=-1.0, in1=empty[:, :],
                                            op0=ALU.add, op1=ALU.add))
                link(v.tensor_copy(token_at[:, :], listed[:, :]))

        X1_SLOTS = 2
        gamma_bc, beta_bc = route_sb("gamma_bc", [P, D]), route_sb("beta_bc", [P, D])
        x1_s = w_raw
        const_in, shifted = sem("f_const"), sem("f_shift")
        x1_in = [sem(f"f_x{i}") for i in range(X1_SLOTS)]

        def load_x1(sp, m):
            sp.dma_start(x1_s[:rows(m), m % X1_SLOTS, :], x1_dram[m * P:m * P + rows(m), :])\
                .then_inc(x1_in[m % X1_SLOTS], 16)

        def shift(pool, m):
            pool.wait_ge(x1_in[m % X1_SLOTS], 16 * (m // X1_SLOTS + 1))
            at = x1_s[:rows(m), m % X1_SLOTS, :]
            pool.tensor_tensor(at, at, beta_bc[:rows(m), :], ALU.add).then_inc(shifted, 1)

        with ExitStack() as stage:
            def ssem(name):
                return stage.enter_context(nc.semaphore(name))

            def ssb(name, shape, dt=F32):
                return stage.enter_context(nc.sbuf_tensor(name, shape, dt))

            tT_hi, tT_lo = ssb("tT_hi", [P, 2, KD, P], F32R), ssb("tT_lo", [P, 2, KD, P], F32R)
            h_raw = ssb("h_raw", [P, 2, F])
            hT_s = ssb("hT_s", [P, 2, KF, P])
            hT_hi, hT_lo = ssb("hT_hi", [P, 2, KF, P], F32R), ssb("hT_lo", [P, 2, KF, P], F32R)
            o_s = ssb("o_s", [P, 2, D])
            b2_bc = ssb("b2_bc", [P, D])
            at_s = ssb("at_s", [P, 2], I32)
            gate_w2 = ssb("gate_w2", [1, 2])
            t_in, t_free = [ssem("e_t0"), ssem("e_t1")], ssem("e_tfree")
            raw_hi, raw_lo = ssem("e_rawhi"), ssem("e_rawlo")
            b2_in, copied, cleared = ssem("e_b2"), ssem("e_copied"), ssem("e_cleared")
            s1_done, h_copied, th_done, relu_done, h_hi, h_lo = (
                ssem("e_s1"), ssem("e_hcopy"), ssem("e_th"), ssem("e_relu"), ssem("e_hhi"), ssem("e_hlo"))
            t_hi, t_lo, s2_done, o_ready = ssem("e_thi"), ssem("e_tlo"), ssem("e_s2"), ssem("e_oready")
            o_stored = ssem("e_ostored")
            block = stage.enter_context(nc.Block())
            LAST = BLOCKS_T - 1

            @block.sync
            def _(sp):
                def weights(b):
                    e = expert(sp, b)
                    if not isinstance(b, int):
                        for q in range(RAW):
                            sp.wait_ge(raw_hi, RAW * b + q + 1 - RAW)
                            sp.wait_ge(raw_lo, RAW * b + q + 1 - RAW)
                            load_expert(sp, e, q)
                    wait_after_first(sp, o_ready, 4 * b)
                    sp.dma_start(b2_bc[:, :], b2[bass.ds(e, 1), :].to_broadcast([P, D])).then_inc(b2_in, 16)
                weights(0)
                sp.dma_start(gamma_bc[:, :], gamma[0:1, :].to_broadcast([P, D])).then_inc(const_in, 16)
                sp.dma_start(beta_bc[:, :], beta[0:1, :].to_broadcast([P, D])).then_inc(const_in, 16)
                for m in range(X1_SLOTS):
                    load_x1(sp, m)
                with sp.Fori(1, BLOCKS_T) as b:
                    weights(b)

            @block.gpsimd
            def _(pool):
                pool.memset(gate_w2[:, :], 0.0).then_inc(cleared, 1)
                pool.wait_ge(cleared, 1)

                def gather(b):
                    wait_after_first(pool, t_free, 2 * b)
                    for a in range(2):
                        wait_after_first(pool, t_in[a], 16 * b)
                    pool.tensor_copy(at_s[:, :], token_at[:, bass.ds(2 * b, 2)]).then_inc(copied, 1)
                    pool.wait_ge(copied, b + 1)
                    pool.tensor_tensor(gate_w2[:, 1:2], gate_w2[:, 0:1], gate_w2[:, 0:1], ALU.add)
                    for a in range(2):
                        pool.indirect_dma_start(t_s[:, a, :], None, t_dram,
                                                IndirectOffsetOnAxis(ap=at_s[:, a:a + 1], axis=0),
                                                bounds_check=N - 1, oob_is_err=False).then_inc(t_in[a], 16)
                gather(0)
                gather(1)
                pool.wait_ge(const_in, 32)
                for m in range(X1_SLOTS):
                    shift(pool, m)
                with pool.Fori(2, BLOCKS_T) as b:
                    gather(b)

            def e_hi_piece(act, b, q):
                act.wait_ge(raw_in[q], 16 * b + 16)
                act.activation(w_hi[:, q // PIECES, (q % PIECES) * PIECE:(q % PIECES + 1) * PIECE],
                               e_raw[:, q, :], ACT.Copy).then_inc(raw_hi, 1)

            def e_lo_piece(v, b, q):
                at = slice((q % PIECES) * PIECE, (q % PIECES + 1) * PIECE)
                v.wait_ge(raw_hi, 2 * PIECES * b + q + 1)
                v.tensor_tensor(w_lo[:, q // PIECES, at], e_raw[:, q, :], w_hi[:, q // PIECES, at].bitcast(F32),
                                ALU.subtract).then_inc(raw_lo, 1)

            @block.scalar
            def _(act):
                def t_parts(b):
                    for a in range(2):
                        act.wait_ge(t_free, 2 * b + a + 1)
                        for q in range(2):
                            act.activation(tT_hi[:, a, 4 * q:4 * q + 4, :], four(2 + 2 * a + q, P), ACT.Copy).then_inc(t_hi, 1)

                def body(b, last=False):
                    e = expert(act, b)
                    act.activation(b1_here[:, :], b1_sb[:, bass.ds(e, 1), :].rearrange("p o f -> p (o f)"), ACT.Copy)\
                        .then_inc(b1_copied, 1)
                    wait_after_first(act, s2_done, 4 * b)
                    if not isinstance(b, int) or b > 0:
                        for q in range(PIECES, 2 * PIECES):
                            e_hi_piece(act, b, q)
                    act.wait_ge(b1_copied, b + 1)
                    for a in range(2):
                        act.wait_ge(s1_done, 2 * b + a + 1)
                        act.activation(h_raw[:, a, :], bank[6 + a][:, :], ACT.Copy).then_inc(h_copied, 1)
                        act.wait_ge(th_done, 2 * b + a + 1)
                        wait_after_first(act, h_lo, 2 * b - 1 + a)
                        for f in range(KF):
                            i = act.activation(hT_s[:, a, f, :], bank[6 + a][:, f * P:(f + 1) * P], ACT.Relu,
                                               bias=b1_here[:, f:f + 1])
                        i.then_inc(relu_done, 1)
                        act.wait_ge(relu_done, 2 * b + a + 1)
                        act.activation(hT_hi[:, a, :, :], hT_s[:, a, :, :], ACT.Copy).then_inc(h_hi, 1)
                    if not last:
                        t_parts(b + 1)
                        for q in range(PIECES):
                            e_hi_piece(act, b + 1, q)
                    act.wait_ge(o_ready, 4 * b + 4)
                    act.dma_start(o_dram[bass.ds(b * BLOCK_T, BLOCK_T), :].rearrange("(a p) d -> p a d", p=P),
                                  o_s[:, :, :]).then_inc(o_stored, 16)

                for q in range(2 * PIECES):
                    e_hi_piece(act, 0, q)
                t_parts(0)
                body(0)
                with act.Fori(1, LAST) as b:
                    body(b)
                body(LAST, last=True)
                act.wait_ge(o_stored, 16 * BLOCKS_T)

            @block.vector
            def _(v):
                def t_parts(b):
                    for a in range(2):
                        for q in range(2):
                            v.wait_ge(t_hi, 4 * b + 2 * a + q + 1)
                            v.tensor_tensor(tT_lo[:, a, 4 * q:4 * q + 4, :], four(2 + 2 * a + q, P),
                                            tT_hi[:, a, 4 * q:4 * q + 4, :].bitcast(F32), ALU.subtract).then_inc(t_lo, 1)

                def body(b, last=False):
                    if not isinstance(b, int) or b > 0:
                        for q in range(PIECES, 2 * PIECES):
                            e_lo_piece(v, b, q)
                    for a in range(2):
                        v.wait_ge(h_hi, 2 * b + a + 1)
                        v.tensor_tensor(hT_lo[:, a, :, :], hT_s[:, a, :, :], hT_hi[:, a, :, :].bitcast(F32), ALU.subtract)\
                            .then_inc(h_lo, 1)
                    if not last:
                        t_parts(b + 1)
                        for q in range(PIECES):
                            e_lo_piece(v, b + 1, q)
                    v.wait_ge(b2_in, 16 * b + 16)
                    wait_after_first(v, o_stored, 16 * b)
                    for a in range(2):
                        for q in range(2):
                            v.wait_ge(s2_done, 4 * b + 2 * a + q + 1)
                            v.tensor_tensor(o_s[:, a, q * HALF:(q + 1) * HALF], bank[2 * a + q][:, :],
                                            b2_bc[:, q * HALF:(q + 1) * HALF], ALU.add).then_inc(o_ready, 1)

                for q in range(2 * PIECES):
                    e_lo_piece(v, 0, q)
                t_parts(0)
                body(0)
                with v.Fori(1, LAST) as b:
                    body(b)
                body(LAST, last=True)

            @block.tensor
            def _(pe):
                def token_tile(b, a):
                    pe.wait_ge(t_in[a], 16 * b + 16)
                    for k in range(KD):
                        i = transpose(pe, bank[2 + 2 * a + k // 4][:, (k % 4) * P:(k % 4 + 1) * P],
                                      t_s[:, a, k * P:(k + 1) * P])
                    i.then_inc(t_free, 1)

                def hidden_transposed(b, a):
                    pe.wait_ge(h_copied, 2 * b + a + 1)
                    for f in range(KF):
                        i = transpose(pe, bank[6 + a][:, f * P:(f + 1) * P], h_raw[:, a, f * P:(f + 1) * P])
                    i.then_inc(th_done, 1)

                def body(b, last=False):
                    pe.wait_ge(raw_hi, 2 * PIECES * b + PIECES)
                    pe.wait_ge(raw_lo, 2 * PIECES * b + PIECES)
                    pe.wait_ge(t_lo, 4 * b + 4)
                    wait_after_first(pe, relu_done, 2 * b)
                    for a in range(2):
                        n = 0
                        for x_, y_ in ((tT_hi, w_hi), (tT_hi, w_lo), (tT_lo, w_hi)):
                            if a == 1 and x_ is tT_lo:
                                hidden_transposed(b, 0)
                            for k in range(KD):
                                i = pe.matmul(bank[6 + a][:, :], x_[:, a, k, :], y_[:, 0, k * F:(k + 1) * F],
                                              start=(n == 0), stop=(n == 3 * KD - 1))
                                n += 1
                        i.then_inc(s1_done, 1)
                    wait_after_first(pe, o_ready, 4 * b)
                    if not last:
                        for a in range(2):
                            token_tile(b + 1, a)
                    hidden_transposed(b, 1)
                    pe.wait_ge(raw_hi, 2 * PIECES * (b + 1))
                    pe.wait_ge(raw_lo, 2 * PIECES * (b + 1))
                    for a in range(2):
                        pe.wait_ge(h_lo, 2 * b + a + 1)
                        if a == 1 and not last:
                            pe.wait_ge(t_lo, 4 * b + 6)
                        for q in range(2):
                            n = 0
                            for x_, y_ in ((hT_hi, w_hi), (hT_hi, w_lo), (hT_lo, w_hi)):
                                for k in range(KF):
                                    i = pe.matmul(bank[2 * a + q][:, :], x_[:, a, k, :],
                                                  y_[:, 1, k * D + q * HALF:k * D + (q + 1) * HALF],
                                                  start=(n == 0), stop=(n == 3 * KF - 1))
                                    n += 1
                            i.then_inc(s2_done, 1)

                token_tile(0, 0)
                token_tile(0, 1)
                body(0)
                with pe.Fori(1, LAST) as b:
                    body(b)
                body(LAST, last=True)

        with ExitStack() as stage:
            def ssem(name):
                return stage.enter_context(nc.semaphore(name))

            def ssb(name, shape, dt=F32):
                return stage.enter_context(nc.sbuf_tensor(name, shape, dt))

            SL = 4
            o_in = ssb("o_in", [P, SL, 2, D])
            o_got = [ssem(f"f_o{i}") for i in range(SL)]
            var_ready, std_ready, combined, centred, scaled, y_ready = (
                ssem("f_var"), ssem("f_std"), ssem("f_comb"), ssem("f_cent"), ssem("f_scaled"), ssem("f_y"))
            stored = ssem("f_stored")
            block = stage.enter_context(nc.Block())

            @block.sync
            def _(sp):
                for m in range(TILES):
                    sp.wait_ge(y_ready, m + 1)
                    if m + X1_SLOTS < TILES:
                        load_x1(sp, m + X1_SLOTS)
                    sp.dma_start(out[m * P:m * P + rows(m), :], acc[:rows(m), m, :]).then_inc(stored, 16)
                sp.wait_ge(stored, 16 * TILES)

            @block.gpsimd
            def _(pool):
                def gather(m):
                    a, rm = m % SL, rows(m)
                    if m >= SL:
                        pool.wait_ge(combined, m - SL + 1)
                    for k in range(2):
                        c = k * TILES + m
                        pool.indirect_dma_start(o_in[:rm, a, k, :], None, o_dram,
                                                IndirectOffsetOnAxis(ap=place_i[:rm, c:c + 1], axis=0))\
                            .then_inc(o_got[a], 16)

                for m in range(SL):
                    gather(m)
                for m in range(TILES):
                    if m + SL < TILES:
                        gather(m + SL)
                    if m >= X1_SLOTS:
                        shift(pool, m)
                    pool.wait_ge(scaled, m + 1)
                    pool.wait_ge(shifted, m + 1)
                    o = acc[:rows(m), m, :]
                    pool.tensor_tensor(o, o, x1_s[:rows(m), m % X1_SLOTS, :], ALU.add).then_inc(y_ready, 1)

            @block.scalar
            def _(act):
                for s in range(TILES + 1):
                    if s < TILES:
                        act.wait_ge(var_ready, s + 1)
                        act.activation(rs[:rows(s), s % 2, 1:2], rs[:rows(s), s % 2, 0:1], ACT.Sqrt).then_inc(std_ready, 1)
                    if s >= 1:
                        m = s - 1
                        act.wait_ge(centred, m + 1)
                        o = acc[:rows(m), m, :]
                        act.activation(o, o, ACT.Copy, scale=rs[:rows(m), m % 2, 3:4]).then_inc(scaled, 1)

            @block.vector
            def _(v):
                link = chained(v)

                for s in range(TILES + 1):
                    if s < TILES:
                        rm, slot, o = rows(s), s % SL, acc[:rows(s), s, :]
                        v.wait_ge(o_got[slot], 32 * (s // SL + 1))
                        for k in range(2):
                            i = v.scalar_tensor_tensor(out=o, in0=o_in[:rm, slot, k, :],
                                                       scalar=weight_of[:rm, k, s:s + 1],
                                                       in1=o, op0=ALU.mult, op1=ALU.add)
                            if k == 0:
                                link(i)
                        i.then_inc(combined, 1)
                        v.wait_ge(combined, s + 1)
                        norm_stats(v, link, o, s % 2, rm, var_ready)
                    if s >= 1:
                        m = s - 1
                        rm, a, o = rows(m), m % 2, acc[:rows(m), m, :]
                        v.wait_ge(std_ready, m + 1)
                        rstd(v, link, a, rm, rs[:rm, a, 3:4])
                        v.scalar_tensor_tensor(out=o, in0=o, scalar=aggr[:rm, a, 0:1], in1=gamma_bc[:rm, :],
                                               op0=ALU.subtract, op1=ALU.mult).then_inc(centred, 1)


_OUTS = [((N, D), "float32")]


def kernel(**inputs):
    import numpy as np
    import concourse.bacc as bacc
    from concourse.bass_utils import run_bass_kernel_spmd as run

    def a(name):
        return np.ascontiguousarray(np.asarray(inputs[name]))

    def halves(w):
        return [w[:, h * HALF:(h + 1) * HALF].reshape(-1, P, HALF).transpose(1, 0, 2).reshape(P, -1)
                for h in range(2)]

    weight, root, gate = a("L0_gnn_weight"), a("L0_gnn_root"), a("L0_gnn_w_gate")
    w1, w2 = a("L0_ffn_W1"), a("L0_ffn_W2")
    chunks = []
    for r in range(R):
        chunks += halves(weight[r])
    chunks += halves(root) + halves(gate[D:]) + halves(gate[:D])
    for e in range(E):
        chunks.append(w1[e].T.reshape(KD, P, F).transpose(1, 0, 2).reshape(P, -1))
        chunks.append(w2[e].T.reshape(KF, P, D).transpose(1, 0, 2).reshape(P, -1))
    arrays = {
        "x": a("x"),
        "src": a("src").reshape(EP, EC), "dst": a("dst").reshape(EP, EC),
        "etype": a("edge_type_8").reshape(EP, EC),
        "wchunks": np.concatenate(chunks),
        "bias": a("L0_gnn_bias").reshape(1, D), "b_gate": a("L0_gnn_b_gate").reshape(1, D),
        "wr": np.ascontiguousarray(a("L0_ffn_Wr").T.reshape(KD, P, E).transpose(1, 0, 2)),
        "br": a("L0_ffn_br").reshape(1, E),
        "b1": np.ascontiguousarray(a("L0_ffn_b1").reshape(E, KF, P).transpose(2, 0, 1)),
        "b2": a("L0_ffn_b2"),
        "gamma": a("L0_ffn_gamma").reshape(1, D), "beta": a("L0_ffn_beta").reshape(1, D),
    }
    nc = bacc.Bacc("TRN2", target_bir_lowering=False, num_devices=1, dynamic_dma_scratch_size=8192)
    args, feed = [], {}
    for name, v in arrays.items():
        feed[f"in_{name}"] = v
        args.append(nc.dram_tensor(f"in_{name}", v.shape, mybir.dt.from_np(v.dtype), kind="ExternalInput").ap())
    args.append(nc.dram_tensor("out_0", _OUTS[0][0], F32, kind="ExternalOutput").ap())
    program(nc, *args)
    r = run(nc, [feed], core_ids=[0])
    return r.results[0]["out_0"]
```
